# Optimizing a Trainium2 kernel written in Bass

```python
import numpy as np
import jax
import jax.numpy as jnp

def _softmax(x, axis=-1):
    return jax.nn.softmax(x, axis=axis)

def _gelu(x):
    return jax.nn.gelu(x, approximate=True)

def _silu(x):
    return jax.nn.silu(x)

def _sigmoid(x):
    return jax.nn.sigmoid(x)

def _layernorm(x, axis=-1, eps=1e-05):
    m = jnp.mean(x, axis=axis, keepdims=True)
    v = jnp.var(x, axis=axis, keepdims=True)
    return (x - m) / jnp.sqrt(v + eps)

def _scatter_add(tgt, idx, src, axis=0):
    return tgt.at[idx].add(src)

def _segment_sum(src, seg, n):
    return jax.ops.segment_sum(src, seg, n)
kernel_name = 'mk_gnn_ffn_d2_gnn_r8_6d3f58'

def setup_inputs(seed: int=0):
    np.random.seed(seed)
    _w = jnp.asarray

    def _rec_inputs():
        import jax
        import jax.numpy as jnp
        _gk = jax.random.key(seed)
        x = -8.776e-05 + 1 * jax.random.normal(jax.random.fold_in(_gk, 1), (1250, 512), jnp.float32)
        _s = jax.random.randint(jax.random.fold_in(_gk, 2), (20000,), 0, 1250, jnp.int32)
        _d = jax.random.randint(jax.random.fold_in(_gk, 3), (20000,), 0, 1250, jnp.int32)
        _loop = jnp.arange(1250, dtype=jnp.int32)
        src = jnp.concatenate([_s, _d, _loop])
        dst = jnp.concatenate([_d, _s, _loop])
        _o = jnp.argsort(dst, stable=True)
        src = src[_o]
        dst = dst[_o]
        edge_attr_512 = -8.513e-05 + 0.999844 * jax.random.normal(jax.random.fold_in(_gk, 11), (41250, 512), jnp.float32)
        return (x, src, dst, edge_attr_512)
    x, src, dst, edge_attr_512 = _rec_inputs()

    def _L0_gnn_setup():
        import jax, jax.numpy as jnp
        import numpy as np
        N = 1250
        E = 20000
        D = 512
        key = jax.random.key(seed)
        k1, k2, k3, k4, k5 = jax.random.split(key, 5)
        node_tokens = jax.random.normal(k1, (N, D), dtype=jnp.float32)
        relation_tokens = jax.random.normal(k2, (E, D), dtype=jnp.float32)
        edge_index = jax.random.randint(k3, (2, E), 0, N, dtype=jnp.int64)
        lim_m = float(np.sqrt(6.0 / (D + D)))
        Wm = jax.random.uniform(k4, (D, D), minval=-lim_m, maxval=lim_m, dtype=jnp.float32)
        bm = jnp.zeros((D,), dtype=jnp.float32)
        lim_u = float(np.sqrt(6.0 / (2 * D + D)))
        Wu = jax.random.uniform(k5, (D, 2 * D), minval=-lim_u, maxval=lim_u, dtype=jnp.float32)
        bu = jnp.zeros((D,), dtype=jnp.float32)
        gamma = jnp.ones((D,), dtype=jnp.float32)
        beta = jnp.zeros((D,), dtype=jnp.float32)
        return {'node_tokens': node_tokens, 'relation_tokens': relation_tokens, 'edge_index': edge_index, 'num_nodes': N, 'Wm': Wm, 'bm': bm, 'Wu': Wu, 'bu': bu, 'gamma': gamma, 'beta': beta}
    _L0_gnn_all = _L0_gnn_setup()
    _L0_gnn_in = {k: v for k, v in _L0_gnn_all.items() if k in ('Wm', 'bm', 'Wu', 'bu', 'gamma', 'beta')}
    del _L0_gnn_all

    def _L0_ffn_setup():
        import jax, jax.numpy as jnp
        import numpy as np
        D_MODEL = 512
        DFF = 256
        E = 8
        K = 2
        B, N = (2, 256)
        key = jax.random.key(seed)
        ks = jax.random.split(key, 6)
        x = jax.random.normal(ks[0], (B, N, D_MODEL), dtype=jnp.float32)
        router_w = jax.random.normal(ks[1], (E, D_MODEL), dtype=jnp.float32) * 0.01
        lim1 = float(np.sqrt(6.0 / (D_MODEL + DFF)))
        w1_all = jax.random.uniform(ks[2], (E, DFF, D_MODEL), minval=-lim1, maxval=lim1, dtype=jnp.float32)
        w2_all = jax.random.uniform(ks[3], (E, D_MODEL, DFF), minval=-lim1, maxval=lim1, dtype=jnp.float32)
        b1_all = jax.random.normal(ks[4], (E, DFF), dtype=jnp.float32) * 0.01
        b2_all = jax.random.normal(ks[5], (E, D_MODEL), dtype=jnp.float32) * 0.01
        return {'x': x, 'router_w': router_w, 'w1_all': w1_all, 'b1_all': b1_all, 'w2_all': w2_all, 'b2_all': b2_all}
    _L0_ffn_all = _L0_ffn_setup()
    _L0_ffn_in = {k: v for k, v in _L0_ffn_all.items() if k in ('router_w', 'w1_all', 'b1_all', 'w2_all', 'b2_all')}
    del _L0_ffn_all

    def _L1_gnn_setup():
        import jax, jax.numpy as jnp
        import numpy as np
        BN_EPS = 1e-05

        def batch_norm(h, gamma, beta):
            mu = jnp.mean(h, axis=0)
            var = jnp.var(h, axis=0)
            return (h - mu) * jax.lax.rsqrt(var + BN_EPS) * gamma + beta
        key = jax.random.key(seed)
        ks = jax.random.split(key, 6)
        N, E, dim = (6250, 200000, 512)
        hidden = dim * 2
        x = jax.random.normal(ks[0], (N, dim), dtype=jnp.float32)
        edge_index = jax.random.randint(ks[1], (2, E), 0, N, dtype=jnp.int64)
        s1 = 1.0 / np.sqrt(dim)
        s2 = 1.0 / np.sqrt(hidden)
        return {'x': x, 'edge_index': edge_index, 'eps': jnp.float32(0.0), 'W1': jax.random.uniform(ks[2], (dim, hidden), jnp.float32, -s1, s1), 'b1': jnp.zeros((hidden,), jnp.float32), 'g1': jnp.ones((hidden,), jnp.float32), 'be1': jnp.zeros((hidden,), jnp.float32), 'W2': jax.random.uniform(ks[3], (hidden, dim), jnp.float32, -s2, s2), 'b2': jnp.zeros((dim,), jnp.float32), 'g2': jnp.ones((dim,), jnp.float32), 'be2': jnp.zeros((dim,), jnp.float32)}
    _L1_gnn_all = _L1_gnn_setup()
    _L1_gnn_in = {k: v for k, v in _L1_gnn_all.items() if k in ('eps', 'W1', 'b1', 'g1', 'be1', 'W2', 'b2', 'g2', 'be2')}
    del _L1_gnn_all

    def _L1_ffn_setup():
        import jax, jax.numpy as jnp
        import numpy as np
        B, S, D, F, E = (8, 512, 512, 256, 8)
        INIT_LAMBDA = 0.2
        LN_EPS = 1e-05
        LN_MERGE = 0.03
        key = jax.random.key(seed)
        ks = jax.random.split(key, 12)
        n = lambda k, shp, s=1.0: jax.random.normal(k, shp, dtype=jnp.float32) * s
        return {'hidden_states': n(ks[0], (B, S, D)), 'gfc1_w': n(ks[1], (D, D), 0.01), 'gfc1_b': jnp.zeros((D,), jnp.float32), 'gfc2_w': n(ks[2], (E, D), 0.01), 'gfc2_b': jnp.full((E,), INIT_LAMBDA, dtype=jnp.float32), 'W1': n(ks[3], (F, D), 0.02), 'b1': jnp.zeros((F,), jnp.float32), 'W2': n(ks[4], (D, F), 0.02), 'b2': jnp.zeros((D,), jnp.float32), 'ln_g': jnp.ones((D,), jnp.float32), 'ln_b': jnp.zeros((D,), jnp.float32), 'tv_W1': n(ks[5], (E, F, D), 0.02), 'tv_b1': n(ks[6], (E, F), 0.02), 'tv_W2': n(ks[7], (E, D, F), 0.02), 'tv_b2': n(ks[8], (E, D), 0.02), 'tv_ln_g': n(ks[9], (E, D), 0.02), 'tv_ln_b': n(ks[10], (E, D), 0.02)}
    _L1_ffn_all = _L1_ffn_setup()
    _L1_ffn_in = {k: v for k, v in _L1_ffn_all.items() if k in ('gfc1_w', 'gfc1_b', 'gfc2_w', 'gfc2_b', 'W1', 'b1', 'W2', 'b2', 'ln_g', 'ln_b', 'tv_W1', 'tv_b1', 'tv_W2', 'tv_b2', 'tv_ln_g', 'tv_ln_b')}
    del _L1_ffn_all
    return {'x': x, 'src': src, 'dst': dst, 'edge_attr_512': edge_attr_512, 'L0_gnn_Wm': _L0_gnn_in['Wm'], 'L0_gnn_bm': _L0_gnn_in['bm'], 'L0_gnn_Wu': _L0_gnn_in['Wu'], 'L0_gnn_bu': _L0_gnn_in['bu'], 'L0_gnn_gamma': _L0_gnn_in['gamma'], 'L0_gnn_beta': _L0_gnn_in['beta'], 'L0_ffn_router_w': _L0_ffn_in['router_w'], 'L0_ffn_w1_all': _L0_ffn_in['w1_all'], 'L0_ffn_b1_all': _L0_ffn_in['b1_all'], 'L0_ffn_w2_all': _L0_ffn_in['w2_all'], 'L0_ffn_b2_all': _L0_ffn_in['b2_all'], 'L1_gnn_eps': _L1_gnn_in['eps'], 'L1_gnn_W1': _L1_gnn_in['W1'], 'L1_gnn_b1': _L1_gnn_in['b1'], 'L1_gnn_g1': _L1_gnn_in['g1'], 'L1_gnn_be1': _L1_gnn_in['be1'], 'L1_gnn_W2': _L1_gnn_in['W2'], 'L1_gnn_b2': _L1_gnn_in['b2'], 'L1_gnn_g2': _L1_gnn_in['g2'], 'L1_gnn_be2': _L1_gnn_in['be2'], 'L1_ffn_gfc1_w': _L1_ffn_in['gfc1_w'], 'L1_ffn_gfc1_b': _L1_ffn_in['gfc1_b'], 'L1_ffn_gfc2_w': _L1_ffn_in['gfc2_w'], 'L1_ffn_gfc2_b': _L1_ffn_in['gfc2_b'], 'L1_ffn_W1': _L1_ffn_in['W1'], 'L1_ffn_b1': _L1_ffn_in['b1'], 'L1_ffn_W2': _L1_ffn_in['W2'], 'L1_ffn_b2': _L1_ffn_in['b2'], 'L1_ffn_ln_g': _L1_ffn_in['ln_g'], 'L1_ffn_ln_b': _L1_ffn_in['ln_b'], 'L1_ffn_tv_W1': _L1_ffn_in['tv_W1'], 'L1_ffn_tv_b1': _L1_ffn_in['tv_b1'], 'L1_ffn_tv_W2': _L1_ffn_in['tv_W2'], 'L1_ffn_tv_b2': _L1_ffn_in['tv_b2'], 'L1_ffn_tv_ln_g': _L1_ffn_in['tv_ln_g'], 'L1_ffn_tv_ln_b': _L1_ffn_in['tv_ln_b']}

def reference(x, src, dst, edge_attr_512, L0_gnn_Wm, L0_gnn_bm, L0_gnn_Wu, L0_gnn_bu, L0_gnn_gamma, L0_gnn_beta, L0_ffn_router_w, L0_ffn_w1_all, L0_ffn_b1_all, L0_ffn_w2_all, L0_ffn_b2_all, L1_gnn_eps, L1_gnn_W1, L1_gnn_b1, L1_gnn_g1, L1_gnn_be1, L1_gnn_W2, L1_gnn_b2, L1_gnn_g2, L1_gnn_be2, L1_ffn_gfc1_w, L1_ffn_gfc1_b, L1_ffn_gfc2_w, L1_ffn_gfc2_b, L1_ffn_W1, L1_ffn_b1, L1_ffn_W2, L1_ffn_b2, L1_ffn_ln_g, L1_ffn_ln_b, L1_ffn_tv_W1, L1_ffn_tv_b1, L1_ffn_tv_W2, L1_ffn_tv_b2, L1_ffn_tv_ln_g, L1_ffn_tv_ln_b):
    import jax
    import jax.numpy as jnp

    def _L0_gnn_ref(node_tokens, relation_tokens, edge_index, num_nodes, Wm, bm, Wu, bu, gamma, beta):
        import jax, jax.numpy as jnp
        import numpy as np
        N = 1250
        E = 20000
        D = 512
        head = edge_index[0]
        tail = edge_index[1]
        msg = node_tokens[head] + relation_tokens
        msg = msg @ Wm.T + bm
        agg = jax.ops.segment_sum(msg, tail, num_segments=num_nodes)
        deg = jax.ops.segment_sum(jnp.ones((msg.shape[0],), dtype=msg.dtype), tail, num_segments=num_nodes)
        agg = agg / jnp.maximum(deg, 1.0)[:, None]
        update_in = jnp.concatenate((node_tokens, agg), axis=-1)
        update = update_in @ Wu.T + bu
        out = node_tokens + jax.nn.gelu(update, approximate=False)
        mean = jnp.mean(out, axis=-1, keepdims=True)
        var = jnp.var(out, axis=-1, keepdims=True)
        return (out - mean) / jnp.sqrt(var + 1e-05) * gamma + beta

    def _L0_ffn_ref(x, router_w, w1_all, b1_all, w2_all, b2_all):
        import jax, jax.numpy as jnp
        import numpy as np
        D_MODEL = 512
        DFF = 256
        E = 8
        K = 2
        B, N = (2, 256)
        Bb, Nn, C = x.shape
        L = Bb * Nn
        x_flat = x.reshape(L, C)
        router_logits = x_flat @ router_w.T
        router_probs = jax.nn.softmax(router_logits, axis=-1)
        expert_weights, expert_indices = jax.lax.top_k(router_probs, K)
        expert_weights = expert_weights / (jnp.sum(expert_weights, axis=-1, keepdims=True) + 1e-09)
        h = jax.nn.relu(jnp.einsum('lc,efc->lef', x_flat, w1_all) + b1_all[None])
        out_all = jnp.einsum('lef,ecf->lec', h, w2_all) + b2_all[None]
        out_sel = jnp.take_along_axis(out_all, expert_indices[:, :, None], axis=1)
        final = jnp.sum(out_sel * expert_weights[:, :, None], axis=1)
        return final.reshape(Bb, Nn, C)

    def _L1_gnn_ref(x, edge_index, eps, W1, b1, g1, be1, W2, b2, g2, be2):
        import jax, jax.numpy as jnp
        import numpy as np
        BN_EPS = 1e-05

        def batch_norm(h, gamma, beta):
            mu = jnp.mean(h, axis=0)
            var = jnp.var(h, axis=0)
            return (h - mu) * jax.lax.rsqrt(var + BN_EPS) * gamma + beta
        N = x.shape[0]
        src, dst = (edge_index[0], edge_index[1])
        agg = jax.ops.segment_sum(x[src], dst, num_segments=N)
        h = (1.0 + eps) * x + agg
        h = jax.nn.relu(batch_norm(h @ W1 + b1, g1, be1))
        h = h @ W2 + b2
        h = jax.nn.relu(batch_norm(h, g2, be2))
        return x + h

    def _L1_ffn_ref(hidden_states, gfc1_w, gfc1_b, gfc2_w, gfc2_b, W1, b1, W2, b2, ln_g, ln_b, tv_W1, tv_b1, tv_W2, tv_b2, tv_ln_g, tv_ln_b):
        import jax, jax.numpy as jnp
        import numpy as np
        B, S, D, F, E = (8, 512, 512, 256, 8)
        INIT_LAMBDA = 0.2
        LN_EPS = 1e-05
        LN_MERGE = 0.03
        x = hidden_states
        gh = jax.nn.relu(jnp.einsum('bsd,hd->bsh', x, gfc1_w) + gfc1_b)
        g = (jnp.einsum('bsh,eh->bse', gh, gfc2_w) + gfc2_b).mean(axis=1)
        W1m = W1 + jnp.einsum('be,efd->bfd', g, tv_W1)
        b1m = b1 + g @ tv_b1
        W2m = W2 + jnp.einsum('be,edf->bdf', g, tv_W2)
        b2m = b2 + g @ tv_b2
        lng = ln_g + LN_MERGE * (tv_ln_g - ln_g).sum(axis=0)
        lnb = ln_b + LN_MERGE * (tv_ln_b - ln_b).sum(axis=0)
        h = jax.nn.relu(jnp.einsum('bsd,bfd->bsf', x, W1m) + b1m[:, None, :])
        out = jnp.einsum('bsf,bdf->bsd', h, W2m) + b2m[:, None, :]
        res = x + out
        mu = res.mean(axis=-1, keepdims=True)
        var = res.var(axis=-1, keepdims=True)
        return (res - mu) * jax.lax.rsqrt(var + LN_EPS) * lng + lnb
    edge_index = jnp.stack([src, dst])
    x = x + _L0_gnn_ref(_layernorm(x, axis=-1), edge_attr_512, edge_index, 1250, L0_gnn_Wm, L0_gnn_bm, L0_gnn_Wu, L0_gnn_bu, L0_gnn_gamma, L0_gnn_beta)
    x = x + _L0_ffn_ref(_layernorm(x, axis=-1)[None], L0_ffn_router_w, L0_ffn_w1_all, L0_ffn_b1_all, L0_ffn_w2_all, L0_ffn_b2_all)[0]
    x = x + _L1_gnn_ref(_layernorm(x, axis=-1), edge_index, L1_gnn_eps, L1_gnn_W1, L1_gnn_b1, L1_gnn_g1, L1_gnn_be1, L1_gnn_W2, L1_gnn_b2, L1_gnn_g2, L1_gnn_be2)
    x = x + _L1_ffn_ref(_layernorm(x, axis=-1)[None], L1_ffn_gfc1_w, L1_ffn_gfc1_b, L1_ffn_gfc2_w, L1_ffn_gfc2_b, L1_ffn_W1, L1_ffn_b1, L1_ffn_W2, L1_ffn_b2, L1_ffn_ln_g, L1_ffn_ln_b, L1_ffn_tv_W1, L1_ffn_tv_b1, L1_ffn_tv_W2, L1_ffn_tv_b2, L1_ffn_tv_ln_g, L1_ffn_tv_ln_b)[0]
    return x

_drawn_inputs = setup_inputs


def setup_inputs(seed=0):
    import zlib

    import numpy as np

    out = dict(_drawn_inputs(seed))
    spreads = {'L0_gnn_bm': (0.0, 0.1),
     'L0_gnn_bu': (0.0, 0.1),
     'L0_gnn_gamma': (1.0, 0.2),
     'L0_gnn_beta': (0.0, 0.1),
     'L1_gnn_b1': (0.0, 2.0),
     'L1_gnn_g1': (1.0, 0.2),
     'L1_gnn_be1': (0.0, 0.441),
     'L1_gnn_b2': (0.0, 2.0),
     'L1_gnn_g2': (1.0, 0.2),
     'L1_gnn_be2': (0.0, 0.338),
     'L1_ffn_gfc1_b': (0.0, 0.8),
     'L1_ffn_gfc2_b': (0.20000000298023224, 0.6),
     'L1_ffn_b1': (0.0, 2.0),
     'L1_ffn_b2': (0.0, 2.0),
     'L1_ffn_ln_g': (1.0, 0.2),
     'L1_ffn_ln_b': (0.0, 0.391)}
    factors = {'L0_ffn_b1_all': 28.241,
     'L0_ffn_b2_all': 8.0,
     'L1_ffn_gfc1_w': 8.0,
     'L1_ffn_gfc2_w': 8.0,
     'L1_ffn_W1': 2.674,
     'L1_ffn_tv_W1': 3.869,
     'L1_ffn_tv_b1': 8.0,
     'L1_ffn_tv_W2': 3.372,
     'L1_ffn_tv_b2': 64.0,
     'L1_ffn_tv_ln_g': 64.0,
     'L1_ffn_tv_ln_b': 64.0,
     'L1_ffn_W2': 3.48}
    for name, (base, spread) in spreads.items():
        noise = np.random.default_rng([zlib.crc32(name.encode()), seed]).standard_normal(out[name].shape)
        drawn = base * np.exp(spread * noise) if base else spread * noise
        out[name] = jnp.asarray(drawn.astype(out[name].dtype))
    for name, factor in factors.items():
        out[name] = (out[name] * factor).astype(out[name].dtype)
    return out
```

```python
from contextlib import ExitStack

import concourse.bass as bass
from concourse import mybir

F32 = mybir.dt.float32
F32R = mybir.dt.float32r
F16 = mybir.dt.float16
BF16 = mybir.dt.bfloat16
I32 = mybir.dt.int32
U32 = mybir.dt.uint32
ALU = mybir.AluOpType
ACT = mybir.ActivationFunctionType
AX = mybir.AxisListType.X

P = 128
NODES, D, EDGES = 1250, 512, 41250
TILES, TP = 10, 125
KT = D // P
GROUP = 4
GROUPS = -(-EDGES // (GROUP * P))
CHUNKS = GROUPS * GROUP
EXPERTS, FF = 8, 256
HID = 1024
EPS = 1e-5
MERGE = 0.03
COLS = [(0, 417), (417, 417), (834, 416)]
NC3 = len(COLS)
BANKS = 8

VEC = {}
_at = 0
for _name, _n in [("bm", 4), ("moe_b1", 16), ("b1", 8), ("g1", 8), ("be1", 8), ("b2", 4), ("g2", 4),
                  ("be2", 4), ("gfc1_b", 4)]:
    VEC[_name] = (_at, _at + _n)
    _at += _n
NVEC = _at


def psum_jobs():
    jobs = [("deg", q) for q in range(3)]
    jobs += [("agg_in", c, f) for c in range(NC3) for f in range(KT)]
    jobs += [("agg", c, o) for c in range(NC3) for o in range(KT)]
    for t in range(TILES + 2):
        if t < TILES:
            jobs.append(("update", t))
        if t >= 2:
            jobs.append(("h1_T", t - 2))
    jobs.append(("router",))
    for e in range(EXPERTS):
        jobs += [("moe_hidden", e, m, c) for m in range(2) for c in range(NC3)]
        jobs += [("moe_out", e, t) for t in range(TILES)]
    jobs += [("gate_T", q) for q in range(3)]
    jobs += [("moe_bias", t) for t in range(TILES)]
    jobs += [("gin", c, f) for c in range(NC3) for f in range(KT)]
    jobs += [("up", h, c) for h in range(8) for c in range(NC3)]
    jobs += [("down", o, c) for o in range(KT) for c in range(NC3)]
    for t in range(TILES + 2):
        if t < TILES:
            jobs.append(("gin_T", t))
        if t >= 2:
            jobs.append(("h3_T", t - 2))
    jobs += [("gate_hidden", o, c) for o in range(KT) for c in range(NC3)]
    jobs += [("gates",)] + [("rows", r) for r in range(3)] + [("b1m",)]
    jobs += [("ffn_hidden", m, c) for m in range(2) for c in range(NC3)]
    jobs += [("ffn_out", t) for t in range(TILES)]
    return {job: n for n, job in enumerate(jobs)}


def norm_calls():
    calls = [("h0", t) for t in range(TILES)]
    for t in range(TILES):
        calls += [("update", t), ("x1", t)]
    calls += [("x2", t) for t in range(TILES)] + [("up", h) for h in range(8)] + [("down", h) for h in range(KT)]
    calls += [("x3", t) for t in range(TILES)] + [("y", t) for t in range(TILES)]
    return {call: n for n, call in enumerate(calls)}


def gnn_ffn_kernel(nc, a, out):
    job_number = psum_jobs()
    norm_number = norm_calls()
    with ExitStack() as ctx:
        def sb(name, shape, dt=F32):
            return ctx.enter_context(nc.sbuf_tensor(name, shape, dt))

        def sem(name):
            return ctx.enter_context(nc.semaphore(name))

        X = sb("X", [TP, TILES, D])
        H = sb("H", [TP, TILES, D])
        HT = sb("HT", [P, KT, NODES])
        AT = sb("AT", [P, TILES * NODES])
        U = sb("U", [P, 8 * NODES])
        W = sb("W", [P, 8192])
        RING = sb("RING", [P, 2048])
        rows = sb("rows", [TP, 3, D])
        hi = sb("hi", [P, 2, D], F32R)
        lo = sb("lo", [P, 2, D], F32R)
        dst_hot_r = sb("dst_hot_r", [P, 2, P], F32R)
        ident = sb("ident", [P, P])
        vec = sb("vec", [P, NVEC])
        small = sb("small", [P, 208])
        rng = sb("rng", [2, 16], I32)

        AT3 = AT[0:TP, :].rearrange("p (s n) -> p s n", s=TILES)

        def view(region, at, parts, *shape):
            n = 1
            for s in shape:
                n *= s
            v = region[0:parts, at:at + n]
            if len(shape) == 2:
                return v.rearrange("p (a b) -> p a b", a=shape[0])
            return v

        ZT = view(U, 0, P, KT, NODES)
        UP = KT * NODES
        a_row = view(U, UP, TP, NODES)
        s_row = view(U, UP + 1250, TP, D)
        src_hot = U[:, UP + 1762:UP + 3012].bitcast(BF16).rearrange("p (s n) -> p s n", s=2)
        iota = U[:, UP + 3012:UP + 3637].bitcast(F16)
        dst_hot = U[:, UP + 3638:UP + 3766].bitcast(BF16).rearrange("p (s n) -> p s n", s=2)
        dst_f = view(U, UP + 3766, P, CHUNKS)
        src_f = view(U, UP + 4090, P, CHUNKS)
        ge = U[:, UP + 4414:UP + 4738].bitcast(BF16).rearrange("p (s n) -> p s n", s=2)
        idx = U[:, 0:2 * CHUNKS].bitcast(I32)
        first_g = view(U, 700, TILES, CHUNKS)
        last_g = view(U, 1100, TILES, CHUNKS)
        hit = view(U, 1500, TILES, CHUNKS)
        sign = U[:, 1900:1900 + 11].bitcast(BF16)
        aggT = view(U, UP, P, KT, NODES)
        degB = view(W, 6144, P, NODES)
        recB = view(RING, 0, P, NODES)
        hidden = [view(U, s * 2 * NODES, P, 2, NODES) for s in range(2)]
        gateT = view(U, UP, EXPERTS, NODES)
        gate = view(U, UP + 1300, TP, TILES, EXPERTS)
        probs = view(U, UP + 1400, TP, TILES, EXPERTS)
        top_v = view(U, UP + 1500, TP, TILES, EXPERTS)
        top_i = U[0:TP, UP + 1600:UP + 1680].bitcast(U32).rearrange("p (t e) -> p t e", t=TILES)
        top_f = view(U, UP + 1700, TP, TILES, EXPERTS)
        pick = view(U, UP + 1800, TP, TILES, EXPERTS)
        pick2 = view(U, UP + 1900, TP, TILES, EXPERTS)
        iota8 = sb("iota8", [TP, EXPERTS])
        rtmp = view(U, UP + 2010, TP, TILES)
        rsum = view(U, UP + 2020, TP, TILES)
        rw = view(U, UP + 2040, TP, 2, TILES)
        moe_b2 = view(U, UP + 2100, EXPERTS, D)
        router_w = sb("router_w", [P, KT, EXPERTS])
        UT = view(U, 0, P, 8, NODES)
        eyeps = view(U, UP + 3000, TP, TP)
        w_msg = view(W, 0, P, KT, D)
        w_upd = view(W, 2048, P, 8, D)
        edge_rows = RING[:, :].rearrange("p (s n) -> p s n", s=GROUP)
        upd = [view(U, s * D, TP, D) for s in range(2)]
        act_out = [view(U, (2 + s) * D, TP, D) for s in range(2)]
        deg_eye = view(U, UP, TP, TILES, TP)
        moe_w1 = [view(RING, s * 1024, P, KT, FF) for s in range(2)]
        moe_w2 = [view(W, s * 1024, P, 2, D) for s in range(2)]
        w1 = view(W, 4096, P, KT, HID)
        w2 = view(W, 0, P, 8, D)
        tv_w1 = view(AT, 0, P, EXPERTS, KT * FF)
        gfc1 = view(AT, 8192, P, KT, D)
        ffn_w1 = view(AT, 10240, P, KT * FF)
        ffn_w2 = view(AT, 11264, P, 2 * D)
        tv_w2 = view(W, 0, P, EXPERTS, 2 * D)
        tv_rows = view(RING, 0, EXPERTS + 1, FF + 3 * D)
        gfc2 = view(RING, 1800, P, KT, EXPERTS)
        gfc2_b = view(RING, 1840, 1, EXPERTS)
        ghmB = view(U, 4000, P, KT, P)
        ffn_hidden = view(U, 0, P, 2, NODES)

        psum = [ctx.enter_context(nc.psum_tensor(f"psum{b}", [P, 512], F32)) for b in range(BANKS)]

        ln_st = sb("ln_st", [TP, TILES, 6])
        ln_mv = sb("ln_mv", [TP, TILES, 2])
        ln_rs = sb("ln_rs", [TP, TILES])
        ln_ve = sb("ln_ve", [TP, TILES])
        bn_scale = sb("bn_scale", [P, 12])
        bn_shift = sb("bn_shift", [P, 12])
        degp = sb("degp", [TP, 3, TILES])
        deg = sb("deg", [TP, TILES])
        zeros = sb("zeros", [P, D], BF16)
        ch_stats = small[:, 16:34]
        ch_mv = small[:, 34:36]
        ch_rstd = small[:, 36:37]
        ch_ve = small[:, 37:38]
        minus_half = small[:, 38:39]
        gsum = small[:, 40:52]
        ghm = small[:, 52:56]
        gB = small[:, 56:64]
        g9 = small[:, 64:65]
        lnc = small[0:EXPERTS + 1, 65:66]
        b1m = small[:, 66:68]
        pair_b1 = small[:, 74:78]
        eps1 = small[0:TP, 68:69]
        eps_in = small[0:TP, 69:70]
        last_first = small[0:TILES, 70:72]
        lo_n = small[0:TILES, 72:74]
        ones = small[:, 80:208]
        gB9 = sb("gB9", [EXPERTS + 1, 2, TP])

        def Q(t):
            return job_number[t]

        idx_in, x_in, vec_in, wmsg_in, wupd_in, rows_in = (sem(n) for n in (
            "idx_in", "x_in", "vec_in", "wmsg_in", "wupd_in", "rows_in"))
        consts = sem("consts")
        dve, act, pool = sem("dve_step"), sem("act_step"), sem("pool_step")
        hits = sem("hits")
        hits_used = sem("hits_used")
        hits_done = sem("hits_done")
        range_ready = sem("range_ready")
        range_T = sem("range_T")
        rng_ready = sem("rng_ready")
        h0_ready, h0_T, h0_copied = sem("h0_ready"), sem("h0_T"), sem("h0_copied")
        rows_landed = [sem(f"edge_rows_landed{j}") for j in range(GROUP)]
        hi_ready = [sem(f"hi_ready{j}") for j in range(GROUP)]
        lo_ready = [sem(f"lo_ready{j}") for j in range(GROUP)]
        hot_ready = [sem(f"hot_ready{j}") for j in range(GROUP)]
        chunk_done = [sem(f"chunk_done{j}") for j in range(GROUP)]
        a_copied, s_copied = sem("a_copied"), sem("s_copied")
        a_T, s_T = sem("a_T"), sem("s_T")
        aT_copied, sT_copied = sem("aT_copied"), sem("sT_copied")
        deg_ready = sem("deg_ready")
        bank_full = [sem(f"bank_full{b}") for b in range(BANKS)]
        bank_free = [sem(f"bank_free{b}") for b in range(BANKS)]
        landed = {n: sem(f"{n}_landed") for n in (
            "router_w", "moe_b2", "w1", "w2", "tv_w1", "tv_w2", "ffn_small")}
        moe_in = [sem(f"moe_weights_landed{s}") for s in range(2)]
        deg_diag = sem("deg_diag")
        var_ready, inv_std_ready = sem("var_ready"), sem("inv_std_ready")
        agg_ready, gelu_in, gelu_done = sem("agg_ready"), sem("gelu_in"), sem("gelu_done")
        h1_ready, pair_b1_set = sem("h1_ready"), sem("pair_b1_set")
        logits_in, exp_done, gate_ready = sem("logits_in"), sem("exp_done"), sem("gate_ready")
        diag_done, xh_done, bias_done = sem("diag_done"), sem("xh_done"), sem("bias_done")
        h2_ready, h3_ready = sem("h2_ready"), sem("h3_ready")
        up_norm, up_done = sem("up_norm"), sem("up_done")
        down_norm, down_done = sem("down_norm"), sem("down_done")
        gsum_done, ghm_ready, g_ready = sem("gsum_done"), sem("ghm_ready"), sem("g_ready")
        w1m_ready, w2m_ready, out_ready, stored = (sem(n) for n in (
            "w1m_ready", "w2m_ready", "out_ready", "stored"))

        def full(eng, job, loops=0):
            n = Q(job)
            eng.wait_ge(bank_full[n % BANKS], loops + (n // BANKS + 1))

        def emptied(eng, job):
            n = Q(job)
            eng.wait_ge(bank_free[n % BANKS], n // BANKS + 1)

        def bank(job):
            return psum[Q(job) % BANKS]

        def frees(ins, job):
            ins.then_inc(bank_free[Q(job) % BANKS], 1)

        def tile(ap, t):
            return ap[:, :, t * TP:(t + 1) * TP]

        block = ctx.enter_context(nc.Block())

        @block.sync
        def _(sp):
            sp.dma_start(idx, a["edges"]).then_inc(idx_in, 16)
            for t in range(TILES):
                sp.dma_start(X[:, t, :], a["x"][t * TP:(t + 1) * TP, :]).then_inc(x_in, 16)
            sp.dma_start(vec[:, :], a["vec"]).then_inc(vec_in, 16)
            sp.dma_start(eps_in, a["eps"].broadcast_to([TP, 1])).then_inc(vec_in, 16)
            sp.dma_start(router_w[:, :, :], a["router_w"]).then_inc(landed["router_w"], 16)
            sp.dma_start(w_msg, a["w_msg"]).then_inc(wmsg_in, 16)
            sp.dma_start(w_upd, a["w_upd"]).then_inc(wupd_in, 16)
            for r in range(3):
                sp.dma_start(rows[:, r, :], a["rows"][r:r + 1, :].broadcast_to([TP, D])).then_inc(rows_in, 16)

            done = sp.alloc_register("groups_done")
            sp.reg_mov(done, 0)
            sp.wait_ge(rng_ready, 1)
            with sp.Fori(0, TILES) as t:
                first = sp.value_load(rng[0:1, bass.ds(t, 1)], min_val=0, max_val=GROUPS - 1)
                end = sp.value_load(rng[1:2, bass.ds(t, 1)], min_val=1, max_val=GROUPS)
                with sp.Fori(first, end) as group:
                    n = sp.snap(done, min_val=0, max_val=GROUPS * TILES)
                    for j in range(GROUP):
                        sp.wait_ge(lo_ready[j], n)
                        sp.dma_start(edge_rows[:, j, :],
                                     a["edge_attr"][bass.ds(group * (GROUP * P) + j * P, P), :])\
                          .then_inc(rows_landed[j], 16)
                    sp.reg_add(done, done, 1)

            sp.wait_ge(agg_ready, NC3 * KT)
            full(sp, ("agg", NC3 - 1, KT - 1))
            for s in range(2):
                sp.dma_start(moe_w1[s], a["moe_w1"][s]).then_inc(moe_in[s], 16)
                sp.dma_start(moe_w2[s], a["moe_w2"][s]).then_inc(moe_in[s], 16)
            full(sp, ("update", TILES - 1))
            sp.dma_start(w1, a["w1"]).then_inc(landed["w1"], 16)
            sp.dma_start(moe_b2, a["moe_b2"]).then_inc(landed["moe_b2"], 16)
            with sp.Fori(0, EXPERTS // 2 - 1) as pair:
                for s in range(2):
                    full(sp, ("moe_out", s, TILES - 1), loops=pair * 4)
                    sp.dma_start(moe_w1[s], a["moe_w1"][bass.ds(pair * 2 + (2 + s), 1), :, :, :].rearrange("e p k f -> p (e k) f"))\
                      .then_inc(moe_in[s], 16)
                    sp.dma_start(moe_w2[s], a["moe_w2"][bass.ds(pair * 2 + (2 + s), 1), :, :, :].rearrange("e p k f -> p (e k) f"))\
                      .then_inc(moe_in[s], 16)
            full(sp, ("moe_out", EXPERTS - 1, TILES - 1))
            sp.dma_start(w2, a["w2"]).then_inc(landed["w2"], 16)
            sp.dma_start(tv_rows, a["tv_rows"]).then_inc(landed["ffn_small"], 16)
            sp.dma_start(gfc2, a["gfc2"]).then_inc(landed["ffn_small"], 16)
            sp.dma_start(gfc2_b, a["gfc2_b"]).then_inc(landed["ffn_small"], 16)
            full(sp, ("gin", NC3 - 1, KT - 1))
            sp.dma_start(gfc1, a["gfc1"]).then_inc(landed["tv_w1"], 16)
            sp.dma_start(tv_w1, a["tv_w1"]).then_inc(landed["tv_w1"], 16)
            sp.dma_start(ffn_w1, a["ffn_w1"]).then_inc(landed["tv_w1"], 16)
            sp.dma_start(ffn_w2, a["ffn_w2"]).then_inc(landed["tv_w1"], 16)
            full(sp, ("down", KT - 1, NC3 - 1))
            sp.dma_start(tv_w2, a["tv_w2"]).then_inc(landed["tv_w2"], 16)
            for t in range(TILES):
                sp.wait_ge(out_ready, t + 1)
                sp.dma_start(out[t * TP:(t + 1) * TP, :], X[:, t, :]).then_inc(stored, 16)
            sp.wait_ge(stored, 16 * TILES)

        @block.gpsimd
        def _(pl):
            pl.memset(ident[:, :], 0.0).then_inc(pool, 1)
            pl.memset(minus_half, -0.5).then_inc(pool, 1)
            pl.wait_ge(pool, 2)
            pl.affine_select(out=ident[:, :], in_=ident[:, :], compare_op=ALU.not_equal, fill=1.0, base=0,
                             pattern=[[-1, P]], channel_multiplier=1).then_inc(consts, 1)
            pl.iota(iota[:, :], pattern=[[1, NODES]], base=0, channel_multiplier=0,
                    allow_small_or_imprecise_dtypes=True).then_inc(consts, 1)
            pl.iota(first_g, pattern=[[-1, GROUPS], [0, GROUP]], base=GROUPS, channel_multiplier=0,
                    allow_small_or_imprecise_dtypes=True).then_inc(consts, 1)
            pl.iota(last_g, pattern=[[1, GROUPS], [0, GROUP]], base=1, channel_multiplier=0,
                    allow_small_or_imprecise_dtypes=True).then_inc(consts, 1)
            pl.iota(iota8[:, :], pattern=[[1, EXPERTS]], base=0, channel_multiplier=0,
                    allow_small_or_imprecise_dtypes=True).then_inc(consts, 1)
            pl.wait_ge(vec_in, 32)
            pl.tensor_scalar(eps1, eps_in, 1.0, None, ALU.add).then_inc(pool, 1)

            def inv_std(name, i):
                pl.wait_ge(var_ready, norm_number[name, i] + 1)
                if name in ("up", "down"):
                    o, v = ch_rstd, ch_ve
                else:
                    o, v = ln_rs[:, i:i + 1], ln_ve[:, i:i + 1]
                pl.tensor_tensor(o, v, minus_half[0:v.shape[0], :], ALU.pow).then_inc(inv_std_ready, 1)

            for t in range(TILES):
                inv_std("h0", t)
            done = pl.alloc_register("groups_done")
            pl.reg_mov(done, 0)
            pl.wait_ge(rng_ready, 1)
            with pl.Fori(0, TILES) as t:
                first = pl.value_load(rng[0:1, bass.ds(t, 1)], min_val=0, max_val=GROUPS - 1)
                end = pl.value_load(rng[1:2, bass.ds(t, 1)], min_val=1, max_val=GROUPS)
                with pl.Fori(first, end):
                    n = pl.snap(done, min_val=0, max_val=GROUPS * TILES)
                    for j in range(GROUP):
                        pl.wait_ge(chunk_done[(j + 2) % GROUP], n + (1 if j >= 2 else 0))
                        pl.wait_ge(hi_ready[j], n + 1)
                        pl.tensor_tensor(lo[:, j % 2, :], edge_rows[:, j, :], hi[:, j % 2, :].bitcast(F32),
                                         ALU.subtract).then_inc(lo_ready[j], 1)
                    pl.reg_add(done, done, 1)

            for t in range(TILES):
                inv_std("update", t)
                inv_std("x1", t)
            full(pl, ("update", TILES - 1))
            pl.wait_ge(pool, 3)
            pl.tensor_scalar(eyeps, ident[0:TP, 0:TP], eps1, None, ALU.mult).then_inc(pool, 1)
            pl.wait_ge(pool, 4)
            for t in range(TILES):
                d = AT3[:, t, t * TP:(t + 1) * TP]
                pl.tensor_tensor(d, d, eyeps, ALU.add).then_inc(diag_done, 1)
            for t in range(TILES):
                inv_std("x2", t)
            for t in range(TILES):
                pl.wait_ge(h2_ready, t + 1)
                pl.tensor_tensor(X[:, t, :], X[:, t, :], H[:, t, :], ALU.add).then_inc(xh_done, 1)
            for name, n_out in (("up", 8), ("down", KT), ("x3", TILES)):
                for h in range(n_out):
                    inv_std(name, h)
            emptied(pl, ("rows", 0))
            emptied(pl, ("rows", 2))
            for t in range(TILES):
                pl.wait_ge(h3_ready, t + 1)
                emptied(pl, ("h3_T", t))
                pl.tensor_tensor(H[:, t, :], H[:, t, :], rows[:, 0, :], ALU.add).then_inc(bias_done, 1)
                pl.tensor_tensor(X[:, t, :], X[:, t, :], rows[:, 2, :], ALU.add).then_inc(bias_done, 1)
            for t in range(TILES):
                inv_std("y", t)

        @block.scalar
        def _(ac):
            ac.wait_ge(vec_in, 32)
            for t in range(TILES):
                ac.wait_ge(h0_T, t + 1)
                nc.scalar.activation(tile(HT, t), psum[4 + t % 4][:, 0:KT * TP].rearrange("p (k n) -> p k n", k=KT),
                                     ACT.Copy).then_inc(h0_copied, 1)
            done = ac.alloc_register("groups_done")
            ac.reg_mov(done, 0)
            ac.wait_ge(rng_ready, 1)
            with ac.Fori(0, TILES) as t:
                first = ac.value_load(rng[0:1, bass.ds(t, 1)], min_val=0, max_val=GROUPS - 1)
                end = ac.value_load(rng[1:2, bass.ds(t, 1)], min_val=1, max_val=GROUPS)
                with ac.Fori(first, end):
                    n = ac.snap(done, min_val=0, max_val=GROUPS * TILES)
                    for j in range(GROUP):
                        ac.wait_ge(rows_landed[j], (n + 1) * 16)
                        ac.wait_ge(chunk_done[(j + 2) % GROUP], n + (1 if j >= 2 else 0))
                        nc.scalar.activation(hi[:, j % 2, :], edge_rows[:, j, :], ACT.Copy).then_inc(hi_ready[j], 1)
                    ac.reg_add(done, done, 1)
                n = ac.snap(done, min_val=0, max_val=GROUPS * TILES)
                ac.wait_ge(chunk_done[GROUP - 1], n)
                ac.wait_ge(a_T, t)
                for q, (c, w) in enumerate(COLS):
                    nc.scalar.activation(a_row[:, c:c + w], psum[1 + q][0:TP, 0:w], ACT.Copy,
                                         accum_out=degp[:, q, bass.ds(t, 1)]).then_inc(a_copied, 1)
                ac.wait_ge(a_T, t + 1)
                for q in range(3):
                    s = min(4, TILES - 4 * q)
                    nc.scalar.activation(AT3[:, 4 * q:4 * q + s, bass.ds(t * TP, TP)],
                                         psum[4 + q][0:TP, 0:s * TP].rearrange("p (s n) -> p s n", s=s),
                                         ACT.Copy).then_inc(aT_copied, 1)
            for q in range(3):
                w = min(4, TILES - 4 * q) * TP
                full(ac, ("deg", q))
                frees(nc.scalar.activation(degB[:, q * 500:q * 500 + w], bank(("deg", q))[:, 0:w], ACT.Copy), ("deg", q))
            for t in range(TILES + 2):
                if t < TILES:
                    emptied(ac, ("update", t))
                    nc.scalar.activation(act_out[t % 2], upd[t % 2], ACT.Gelu).then_inc(gelu_done, 1)
                if t >= 2:
                    job = ("h1_T", t - 2)
                    full(ac, job)
                    frees(nc.scalar.activation(tile(HT, t - 2), bank(job)[:, 0:KT * TP].rearrange("p (k n) -> p k n", k=KT),
                                               ACT.Copy), job)
            emptied(ac, ("router",))
            nc.scalar.activation(probs, probs, ACT.Exp).then_inc(exp_done, 1)
            with ac.Fori(0, EXPERTS // 2) as pair:
                n = Q(("moe_hidden", 1, 1, NC3 - 1))
                ac.wait_ge(bank_free[n % BANKS], pair * 4 + (n // BANKS - 3))
                nc.scalar.activation(pair_b1, vec[:, bass.ds(pair * 4 + VEC["moe_b1"][0], 4)], ACT.Copy)\
                    .then_inc(pair_b1_set, 1)
                ac.wait_ge(pair_b1_set, pair + 1)
                for s in range(2):
                    for m in range(2):
                        for q, (c, w) in enumerate(COLS):
                            job = ("moe_hidden", s, m, q)
                            full(ac, job, loops=pair * 4)
                            frees(nc.scalar.activation(
                                hidden[s][:, m, c:c + w], bank(job)[:, 0:w], ACT.Relu,
                                bias=pair_b1[:, 2 * s + m:2 * s + m + 1]), job)
            for q in range(3):
                w = min(4, TILES - 4 * q) * TP
                job = ("gate_T", q)
                full(ac, job)
                frees(nc.scalar.activation(gateT[:, q * 500:q * 500 + w], bank(job)[0:EXPERTS, 0:w], ACT.Copy), job)
            for q, (c, w) in enumerate(COLS):
                for f in range(KT):
                    job = ("gin", q, f)
                    full(ac, job)
                    frees(nc.scalar.activation(HT[:, f, c:c + w], bank(job)[:, 0:w], ACT.Copy), job)
            for name, arr, n_out, normed, finished, off, bvec in (
                    ("up", UT, 8, up_norm, up_done, 0, "b1"), ("down", HT, KT, down_norm, down_done, 8, "b2")):
                b0 = VEC[bvec][0]
                for h in range(n_out + 1):
                    if h < n_out:
                        for q, (c, w) in enumerate(COLS):
                            job = (name, h, q)
                            full(ac, job)
                            frees(nc.scalar.activation(arr[:, h, c:c + w], bank(job)[:, 0:w], ACT.Identity,
                                                       bias=vec[:, b0 + h:b0 + h + 1]), job)
                    if h >= 1:
                        ac.wait_ge(normed, h)
                        nc.scalar.activation(arr[:, h - 1, :], arr[:, h - 1, :], ACT.Relu,
                                             scale=bn_scale[:, off + h - 1:off + h],
                                             bias=bn_shift[:, off + h - 1:off + h]).then_inc(finished, 1)
            for t in range(TILES):
                job = ("h3_T", t)
                full(ac, job)
                frees(nc.scalar.activation(tile(HT, t), bank(job)[:, 0:KT * TP].rearrange("p (k n) -> p k n", k=KT),
                                           ACT.Copy), job)
            g0 = VEC["gfc1_b"][0]
            for o in range(KT):
                for q, (c, w) in enumerate(COLS):
                    job = ("gate_hidden", o, q)
                    full(ac, job)
                    nc.scalar.activation(bank(job)[:, 0:w], bank(job)[:, 0:w], ACT.Relu, bias=vec[:, g0 + o:g0 + o + 1],
                                         accum_out=gsum[:, 3 * o + q:3 * o + q + 1]).then_inc(bank_free[Q(job) % BANKS], 1)
            for r in range(3):
                full(ac, ("rows", r))
                frees(nc.scalar.activation(rows[:, r, :], bank(("rows", r))[0:TP, :], ACT.Copy), ("rows", r))
            full(ac, ("b1m",))
            frees(nc.scalar.activation(b1m, bank(("b1m",))[:, 0:2], ACT.Copy), ("b1m",))
            emptied(ac, ("b1m",))
            for m in range(2):
                for q, (c, w) in enumerate(COLS):
                    job = ("ffn_hidden", m, q)
                    full(ac, job)
                    frees(nc.scalar.activation(ffn_hidden[:, m, c:c + w], bank(job)[:, 0:w], ACT.Relu,
                                               bias=b1m[:, m:m + 1]), job)

        @block.vector
        def _(ve):
            steps = [0]

            def did(ins):
                steps[0] += 1
                ins.then_inc(dve, 1)

            def settle():
                ve.wait_ge(dve, steps[0])

            def chain(ins):
                did(ins)
                settle()

            def layer_norm_stats(src, t):
                chain(nc.vector.bn_stats(ln_st[:, t, :], src))
                chain(nc.vector.bn_aggr(ln_mv[:, t, :], ln_st[:, t, :]))
                nc.vector.tensor_scalar(ln_ve[:, t:t + 1], ln_mv[:, t, 1:2], EPS, None, ALU.add).then_inc(var_ready, 1)

            def normalize(dst, src, name, t):
                ve.wait_ge(inv_std_ready, norm_number[name, t] + 1)
                return nc.vector.tensor_scalar(dst, src, ln_mv[:, t, 0:1], ln_rs[:, t:t + 1], ALU.subtract, ALU.mult)

            did(nc.vector.memset(sign[:, :], 0.0))
            did(nc.vector.memset(ones[:, :], 1.0))
            did(nc.vector.memset(zeros[:, :], 0.0))
            did(nc.vector.memset(g9[:, :], 1.0))
            did(nc.vector.memset(lnc[:, :], 1.0 - EXPERTS * MERGE))
            settle()
            did(nc.vector.memset(sign[:, 10:11], 1.0))
            did(nc.vector.memset(sign[:, 9:10], -1.0))
            did(nc.vector.memset(lnc[0:EXPERTS, :], MERGE))
            ve.wait_ge(idx_in, 16)
            did(nc.vector.tensor_copy(dst_f, idx[:, 0:CHUNKS]))
            chain(nc.vector.tensor_copy(src_f, idx[:, CHUNKS:2 * CHUNKS]))
            for i in range(TILES + 1):
                if i >= 2:
                    ve.wait_ge(hits_used, i - 1)
                nc.vector.tensor_scalar(ge[:, i % 2, :], dst_f, float(i * TP), None, ALU.is_ge).then_inc(hits, 1)
            ve.wait_ge(hits_used, TILES + 1)
            ve.wait_ge(consts, 5)
            for c, g in ((0, first_g), (1, last_g)):
                chain(nc.vector.scalar_tensor_tensor(out=hit, in0=psum[0][0:TILES, 0:CHUNKS], scalar=0.0, in1=g,
                                                     op0=ALU.is_gt, op1=ALU.mult))
                chain(nc.vector.tensor_reduce(last_first[:, c:c + 1], hit, AX, ALU.max))
            chain(nc.vector.tensor_scalar(lo_n[:, 0:1], last_first[:, 0:1], -1.0, float(GROUPS), ALU.mult, ALU.add))
            chain(nc.vector.tensor_scalar(lo_n[:, 0:1], lo_n[:, 0:1], float(GROUPS - 1), None, ALU.min))
            nc.vector.scalar_tensor_tensor(out=lo_n[:, 1:2], in0=lo_n[:, 0:1], scalar=1.0, in1=last_first[:, 1:2],
                                           op0=ALU.add, op1=ALU.max).then_inc(range_ready, 1)
            ve.wait_ge(range_T, 1)
            nc.vector.tensor_copy(rng[:, 0:TILES], psum[1][0:2, 0:TILES]).then_inc(rng_ready, 1)

            ve.wait_ge(x_in, 16 * TILES)
            for t in range(TILES + 1):
                if t < TILES:
                    layer_norm_stats(X[:, t, :], t)
                if t >= 1:
                    normalize(H[:, t - 1, :], X[:, t - 1, :], "h0", t - 1).then_inc(h0_ready, 1)

            done = ve.alloc_register("groups_done")
            ve.reg_mov(done, 0)
            with ve.Fori(0, TILES) as t:
                first = ve.value_load(rng[0:1, bass.ds(t, 1)], min_val=0, max_val=GROUPS - 1)
                end = ve.value_load(rng[1:2, bass.ds(t, 1)], min_val=1, max_val=GROUPS)
                with ve.Fori(first, end) as group:
                    n = ve.snap(done, min_val=0, max_val=GROUPS * TILES)
                    for j in range(GROUP):
                        s = j % 2
                        ve.wait_ge(chunk_done[(j + 2) % GROUP], n + (1 if j >= 2 else 0))
                        at = group * GROUP + j
                        nc.vector.tensor_scalar(src_hot[:, s, :], iota[:, :], src_f[:, bass.ds(at, 1)], None, ALU.is_equal)
                        nc.vector.tensor_scalar(dst_hot[:, s, 0:TP], iota[:, bass.ds(t * TP, TP)],
                                                dst_f[:, bass.ds(at, 1)], None, ALU.is_equal)
                        nc.vector.tensor_scalar(dst_hot_r[:, s, 0:TP], iota[:, bass.ds(t * TP, TP)],
                                                dst_f[:, bass.ds(at, 1)], None, ALU.is_equal).then_inc(hot_ready[j], 1)
                    ve.reg_add(done, done, 1)
                n = ve.snap(done, min_val=0, max_val=GROUPS * TILES)
                ve.wait_ge(chunk_done[GROUP - 1], n)
                ve.wait_ge(s_T, t)
                nc.vector.tensor_copy(s_row, psum[0][0:TP, :]).then_inc(s_copied, 1)
                ve.wait_ge(s_T, t + 1)
                nc.vector.tensor_copy(ZT[:, :, bass.ds(t * TP, TP)],
                                      psum[7][:, 0:KT * TP].rearrange("p (k n) -> p k n", k=KT)).then_inc(sT_copied, 1)
            ve.wait_ge(a_copied, 3 * TILES)
            chain(nc.vector.tensor_tensor(deg[:, :], degp[:, 0, :], degp[:, 1, :], ALU.add))
            chain(nc.vector.tensor_tensor(deg[:, :], deg[:, :], degp[:, 2, :], ALU.add))
            ve.wait_ge(a_T, TILES)
            nc.vector.tensor_tensor(deg_eye, ident[0:TP, 0:TP].unsqueeze(1).broadcast_to([TP, TILES, TP]),
                                    deg[:, :].unsqueeze(2).broadcast_to([TP, TILES, TP]), ALU.mult).then_inc(deg_diag, 1)
            for q, (c, w) in enumerate(COLS):
                for f in range(KT):
                    job = ("agg_in", q, f)
                    full(ve, job)
                    frees(nc.vector.tensor_tensor(ZT[:, f, c:c + w], bank(job)[:, 0:w], ZT[:, f, c:c + w], ALU.add), job)
            for q in range(3):
                emptied(ve, ("deg", q))
            chain(nc.vector.tensor_scalar(recB, degB, 1.0, None, ALU.max))
            chain(nc.vector.reciprocal(recB, recB))
            chain(nc.vector.tensor_tensor(degB, degB, recB, ALU.mult))
            bm0 = VEC["bm"][0]
            ve.wait_ge(vec_in, 32)
            for q, (c, w) in enumerate(COLS):
                for o in range(KT):
                    job = ("agg", q, o)
                    full(ve, job)
                    frees(nc.vector.tensor_tensor(aggT[:, o, c:c + w], bank(job)[:, 0:w], recB[:, c:c + w], ALU.mult), job)
                    emptied(ve, job)
                    nc.vector.scalar_tensor_tensor(out=aggT[:, o, c:c + w], in0=degB[:, c:c + w],
                                                   scalar=vec[:, bm0 + o:bm0 + o + 1], in1=aggT[:, o, c:c + w],
                                                   op0=ALU.mult, op1=ALU.add).then_inc(agg_ready, 1)
            ve.wait_ge(rows_in, 48)
            for t in range(TILES + 2):
                g = act_out[(t - 1) % 2]
                if 1 <= t <= TILES:
                    ve.wait_ge(gelu_done, t)
                    chain(nc.vector.tensor_tensor(g, g, H[:, t - 1, :], ALU.add))
                    layer_norm_stats(g, t - 1)
                if t >= 2:
                    normalize(H[:, t - 2, :], X[:, t - 2, :], "x1", t - 2).then_inc(h1_ready, 1)
                if t < TILES:
                    job = ("update", t)
                    full(ve, job)
                    nc.vector.tensor_tensor(upd[t % 2], bank(job)[0:TP, :], rows[:, 0, :], ALU.add)\
                        .then_inc(bank_free[Q(job) % BANKS], 1)
                if 1 <= t <= TILES:
                    x = X[:, t - 1, :]
                    chain(normalize(g, g, "update", t - 1))
                    chain(nc.vector.tensor_tensor(g, g, rows[:, 1, :], ALU.mult))
                    chain(nc.vector.tensor_tensor(g, g, rows[:, 2, :], ALU.add))
                    chain(nc.vector.tensor_tensor(x, x, g, ALU.add))
                    layer_norm_stats(x, t - 1)
            full(ve, ("router",))
            logits = bank(("router",))[0:TP, 0:TILES * EXPERTS].rearrange("p (t e) -> p t e", t=TILES)

            def per_node(v):
                return v.unsqueeze(2).broadcast_to([TP, TILES, EXPERTS])

            chain(nc.vector.tensor_reduce(rtmp, logits, AX, ALU.max))
            frees(nc.vector.tensor_tensor(probs, logits, per_node(rtmp), ALU.subtract), ("router",))
            ve.wait_ge(exp_done, 1)
            chain(nc.vector.tensor_reduce(rsum, probs, AX, ALU.add))
            chain(nc.vector.reciprocal(rsum, rsum))
            chain(nc.vector.tensor_tensor(probs, probs, per_node(rsum), ALU.mult))
            for t in range(TILES):
                did(nc.vector.max(top_v[:, t, :], probs[:, t, :]))
            settle()
            for t in range(TILES):
                did(nc.vector.max_index(top_i[:, t, :], top_v[:, t, :], probs[:, t, :]))
            did(nc.vector.tensor_tensor(rtmp, top_v[:, :, 0], top_v[:, :, 1], ALU.add))
            settle()
            did(nc.vector.tensor_copy(top_f, top_i))
            chain(nc.vector.tensor_scalar(rtmp, rtmp, 1e-9, None, ALU.add))
            chain(nc.vector.reciprocal(rtmp, rtmp))
            for k in range(2):
                did(nc.vector.tensor_tensor(rw[:, k, :], top_v[:, :, k], rtmp, ALU.mult))
            e8 = iota8[:, :].unsqueeze(1).broadcast_to([TP, TILES, EXPERTS])
            did(nc.vector.tensor_tensor(pick, e8, per_node(top_f[:, :, 0]), ALU.is_equal))
            chain(nc.vector.tensor_tensor(pick2, e8, per_node(top_f[:, :, 1]), ALU.is_equal))
            did(nc.vector.tensor_tensor(pick, pick, per_node(rw[:, 0, :]), ALU.mult))
            chain(nc.vector.tensor_tensor(pick2, pick2, per_node(rw[:, 1, :]), ALU.mult))
            nc.vector.tensor_tensor(gate, pick, pick2, ALU.add).then_inc(gate_ready, 1)
            ve.wait_ge(gate_ready, 1)
            with ve.Fori(0, EXPERTS // 2) as pair:
                for s in range(2):
                    for t in range(TILES):
                        job = ("moe_out", s, t)
                        full(ve, job, loops=pair * 4)
                        frees(nc.vector.scalar_tensor_tensor(
                            out=X[:, t, :], in0=bank(job)[0:TP, :], scalar=gate[:, t, bass.ds(pair * 2 + s, 1)],
                            in1=X[:, t, :], op0=ALU.mult, op1=ALU.add), job)
            for t in range(TILES + 1):
                if t < TILES:
                    job = ("moe_bias", t)
                    full(ve, job)
                    frees(nc.vector.tensor_tensor(X[:, t, :], bank(job)[0:TP, :], X[:, t, :], ALU.add), job)
                    emptied(ve, job)
                    layer_norm_stats(X[:, t, :], t)
                if t >= 1:
                    normalize(H[:, t - 1, :], X[:, t - 1, :], "x2", t - 1).then_inc(h2_ready, 1)
            for name, arr, n_out, normed, off, gv, bv in (("up", UT, 8, up_norm, 0, "g1", "be1"),
                                                          ("down", HT, KT, down_norm, 8, "g2", "be2")):
                for h in range(n_out):
                    for q, (c, w) in enumerate(COLS):
                        emptied(ve, (name, h, q))
                        did(nc.vector.bn_stats(ch_stats[:, 6 * q:6 * q + 6], arr[:, h, c:c + w]))
                    settle()
                    chain(nc.vector.bn_aggr(ch_mv, ch_stats))
                    nc.vector.tensor_scalar(ch_ve, ch_mv[:, 1:2], EPS, None, ALU.add).then_inc(var_ready, 1)
                    ve.wait_ge(inv_std_ready, norm_number[name, h] + 1)
                    sc, sh = bn_scale[:, off + h:off + h + 1], bn_shift[:, off + h:off + h + 1]
                    g0, b0 = VEC[gv][0] + h, VEC[bv][0] + h
                    chain(nc.vector.tensor_tensor(sc, ch_rstd, vec[:, g0:g0 + 1], ALU.mult))
                    chain(nc.vector.tensor_tensor(sh, ch_mv[:, 0:1], sc, ALU.mult))
                    nc.vector.tensor_tensor(sh, vec[:, b0:b0 + 1], sh, ALU.subtract).then_inc(normed, 1)
            for t in range(TILES + 1):
                if t < TILES:
                    job = ("gin_T", t)
                    full(ve, job)
                    ve.wait_ge(xh_done, t + 1)
                    frees(nc.vector.tensor_tensor(X[:, t, :], bank(job)[0:TP, :], X[:, t, :], ALU.add), job)
                    emptied(ve, job)
                    layer_norm_stats(X[:, t, :], t)
                if t >= 1:
                    normalize(H[:, t - 1, :], X[:, t - 1, :], "x3", t - 1).then_inc(h3_ready, 1)
            for o in range(KT):
                for q in range(NC3):
                    emptied(ve, ("gate_hidden", o, q))
            chain(nc.vector.tensor_reduce(ghm, gsum.rearrange("p (o q) -> p o q", o=KT), AX, ALU.add))
            chain(nc.vector.tensor_scalar(ghm, ghm, 1.0 / NODES, None, ALU.mult))
            nc.vector.tensor_copy(ghmB, ghm.unsqueeze(2).broadcast_to([P, KT, P])).then_inc(ghm_ready, 1)
            full(ve, ("gates",))
            did(nc.vector.tensor_copy(gB, bank(("gates",))[:, 0:EXPERTS]))
            frees(nc.vector.tensor_copy(g9[0:EXPERTS, :], bank(("gates",))[0:EXPERTS, EXPERTS:EXPERTS + 1]), ("gates",))
            emptied(ve, ("gates",))
            settle()
            did(nc.vector.tensor_copy(gB9[:, 1, :], lnc.broadcast_to([EXPERTS + 1, TP])))
            nc.vector.tensor_copy(gB9[:, 0, :], g9[0:EXPERTS + 1, :].broadcast_to([EXPERTS + 1, TP])).then_inc(g_ready, 1)
            ve.wait_ge(landed["tv_w1"], 64)
            for w, tv, need, ready in ((ffn_w1, tv_w1, None, w1m_ready), (ffn_w2, tv_w2, "tv_w2", w2m_ready)):
                if need:
                    ve.wait_ge(landed[need], 16)
                for e in range(EXPERTS):
                    ins = nc.vector.scalar_tensor_tensor(out=w, in0=tv[:, e, :], scalar=gB[:, e:e + 1], in1=w,
                                                         op0=ALU.mult, op1=ALU.add)
                    if e < EXPERTS - 1:
                        chain(ins)
                    else:
                        ins.then_inc(ready, 1)
            for t in range(TILES + 1):
                if t < TILES:
                    job = ("ffn_out", t)
                    full(ve, job)
                    ve.wait_ge(bias_done, 2 * t + 2)
                    h = H[:, t, :]
                    frees(nc.vector.tensor_tensor(h, bank(job)[0:TP, :], h, ALU.add), job)
                    emptied(ve, job)
                    layer_norm_stats(h, t)
                if t >= 1:
                    h, x = H[:, t - 1, :], X[:, t - 1, :]
                    chain(normalize(h, h, "y", t - 1))
                    chain(nc.vector.tensor_tensor(h, h, rows[:, 1, :], ALU.mult))
                    nc.vector.tensor_tensor(x, x, h, ALU.add).then_inc(out_ready, 1)

        @block.tensor
        def _(pe):
            def take(job, loops=0):
                n = Q(job)
                if n >= BANKS:
                    pe.wait_ge(bank_free[n % BANKS], loops + n // BANKS)
                return psum[n % BANKS]

            def fills(ins, job):
                ins.then_inc(bank_full[Q(job) % BANKS], 1)

            def product(job, out_ap, pairs, loops=0):
                take(job, loops)
                for i, (l, r) in enumerate(pairs):
                    mm = nc.tensor.matmul(out_ap, l, r, start=(i == 0), stop=(i == len(pairs) - 1))
                fills(mm, job)

            for i in range(TILES + 1):
                pe.wait_ge(hits, i + 1)
                nc.tensor.matmul(psum[0][0:TILES, 0:CHUNKS], sign[:, 10 - i:20 - i], ge[:, i % 2, :],
                                 start=(i == 0), stop=(i == TILES)).then_inc(hits_used, 1)
            pe.wait_ge(consts, 1)
            pe.wait_ge(range_ready, 1)
            nc.tensor.transpose(psum[1][0:2, 0:TILES], lo_n, ident[0:TILES, 0:TILES]).then_inc(range_T, 1)
            for t in range(TILES):
                pe.wait_ge(h0_ready, t + 1)
                if t >= 4:
                    pe.wait_ge(h0_copied, t - 3)
                for f in range(KT):
                    mm = nc.tensor.transpose(psum[4 + t % 4][:, f * TP:(f + 1) * TP], H[:, t, f * P:(f + 1) * P],
                                             ident[0:TP, 0:TP])
                mm.then_inc(h0_T, 1)

            done = pe.alloc_register("groups_done")
            pe.reg_mov(done, 0)
            pe.wait_ge(rng_ready, 1)
            pe.wait_ge(h0_copied, TILES)
            with pe.Fori(0, TILES) as t:
                first = pe.value_load(rng[0:1, bass.ds(t, 1)], min_val=0, max_val=GROUPS - 1)
                end = pe.value_load(rng[1:2, bass.ds(t, 1)], min_val=1, max_val=GROUPS)
                nc.tensor.matmul(psum[0][0:TP, :], zeros[:, 0:TP], zeros[:, 0:D], start=True, stop=False, skip_group_check=True)
                for q, (c, w) in enumerate(COLS):
                    nc.tensor.matmul(psum[1 + q][0:TP, 0:w], zeros[:, 0:TP], zeros[:, 0:w], start=True, stop=False,
                                     skip_group_check=True)
                with pe.Fori(first, end):
                    n = pe.snap(done, min_val=0, max_val=GROUPS * TILES)
                    for j in range(GROUP):
                        s = j % 2
                        pe.wait_ge(hot_ready[j], n + 1)
                        for q, (c, w) in enumerate(COLS):
                            nc.tensor.matmul(psum[1 + q][0:TP, 0:w], dst_hot[:, s, 0:TP], src_hot[:, s, c:c + w],
                                             start=False, stop=False, skip_group_check=True)
                        pe.wait_ge(hi_ready[j], n + 1)
                        nc.tensor.matmul(psum[0][0:TP, :], dst_hot_r[:, s, 0:TP], hi[:, s, :], start=False, stop=False,
                                         skip_group_check=True)
                        pe.wait_ge(lo_ready[j], n + 1)
                        nc.tensor.matmul(psum[0][0:TP, :], dst_hot_r[:, s, 0:TP], lo[:, s, :], start=False, stop=False,
                                         skip_group_check=True).then_inc(chunk_done[j], 1)
                    pe.reg_add(done, done, 1)
                pe.wait_ge(a_copied, (t + 1) * 3)
                pe.wait_ge(aT_copied, t * 3)
                for st in range(TILES):
                    mm = nc.tensor.transpose(psum[4 + st // 4][0:TP, (st % 4) * TP:(st % 4 + 1) * TP],
                                             a_row[:, st * TP:(st + 1) * TP], ident[0:TP, 0:TP])
                mm.then_inc(a_T, 1)
                pe.wait_ge(s_copied, t + 1)
                pe.wait_ge(sT_copied, t)
                for f in range(KT):
                    mm = nc.tensor.transpose(psum[7][:, f * TP:(f + 1) * TP], s_row[:, f * P:(f + 1) * P],
                                             ident[0:TP, 0:TP])
                mm.then_inc(s_T, 1)

            pe.wait_ge(aT_copied, 3 * TILES)
            pe.wait_ge(sT_copied, TILES)
            pe.wait_ge(deg_diag, 1)
            for q in range(3):
                job = ("deg", q)
                b = take(job)
                for i in range(min(4, TILES - 4 * q)):
                    mm = nc.tensor.matmul(b[:, i * TP:(i + 1) * TP], ones[0:TP, :], deg_eye[:, 4 * q + i, :], start=True, stop=True)
                fills(mm, job)
            for q, (c, w) in enumerate(COLS):
                for f in range(KT):
                    job = ("agg_in", q, f)
                    product(job, bank(job)[:, 0:w],
                            [(H[:, s, f * P:(f + 1) * P], AT3[:, s, c:c + w]) for s in range(TILES)])
            pe.wait_ge(wmsg_in, 16)
            for q, (c, w) in enumerate(COLS):
                for o in range(KT):
                    if o == 0:
                        for f in range(KT):
                            emptied(pe, ("agg_in", q, f))
                    job = ("agg", q, o)
                    product(job, bank(job)[:, 0:w],
                            [(w_msg[:, k, o * P:(o + 1) * P], ZT[:, k, c:c + w]) for k in range(KT)])
            pe.wait_ge(wupd_in, 16)
            pe.wait_ge(agg_ready, NC3 * KT)

            def transposed(job, t):
                b = take(job)
                for f in range(KT):
                    mm = nc.tensor.transpose(b[:, f * TP:(f + 1) * TP], H[:, t, f * P:(f + 1) * P], ident[0:TP, 0:TP])
                fills(mm, job)

            for t in range(TILES + 2):
                if t < TILES:
                    job = ("update", t)
                    product(job, bank(job)[0:TP, :],
                            [(src[:, k, t * TP:(t + 1) * TP], w_upd[:, i * KT + k, :])
                             for i, src in enumerate((HT, aggT)) for k in range(KT)])
                if t >= 2:
                    pe.wait_ge(h1_ready, t - 1)
                    transposed(("h1_T", t - 2), t - 2)
            pe.wait_ge(landed["router_w"], 16)
            for t in range(TILES):
                emptied(pe, ("h1_T", t))
            job = ("router",)
            b = take(job)
            for t in range(TILES):
                for k in range(KT):
                    mm = nc.tensor.matmul(b[0:TP, t * EXPERTS:(t + 1) * EXPERTS], HT[:, k, t * TP:(t + 1) * TP],
                                          router_w[:, k, :], start=(k == 0), stop=(k == KT - 1))
            fills(mm, job)
            with pe.Fori(0, EXPERTS // 2) as pair:
                for s in range(2):
                    pe.wait_ge(moe_in[s], pair * 32 + 32)
                    for m in range(2):
                        for q, (c, w) in enumerate(COLS):
                            job = ("moe_hidden", s, m, q)
                            product(job, bank(job)[:, 0:w],
                                    [(moe_w1[s][:, k, m * P:(m + 1) * P], HT[:, k, c:c + w]) for k in range(KT)],
                                    loops=pair * 4)
                    for m in range(2):
                        for q in range(NC3):
                            n = Q(("moe_hidden", s, m, q))
                            pe.wait_ge(bank_free[n % BANKS], pair * 4 + (n // BANKS + 1))
                    for t in range(TILES):
                        job = ("moe_out", s, t)
                        product(job, bank(job)[0:TP, :],
                                [(hidden[s][:, k, t * TP:(t + 1) * TP], moe_w2[s][:, k, :]) for k in range(2)],
                                loops=pair * 4)
            for q in range(3):
                job = ("gate_T", q)
                b = take(job)
                for i in range(min(4, TILES - 4 * q)):
                    mm = nc.tensor.transpose(b[0:EXPERTS, i * TP:(i + 1) * TP], gate[:, 4 * q + i, :], ident[0:TP, 0:TP])
                fills(mm, job)
            pe.wait_ge(landed["moe_b2"], 16)
            for q in range(3):
                emptied(pe, ("gate_T", q))
            for t in range(TILES):
                job = ("moe_bias", t)
                product(job, bank(job)[0:TP, :], [(gateT[:, t * TP:(t + 1) * TP], moe_b2)])
            pe.wait_ge(diag_done, TILES)
            pe.wait_ge(h2_ready, TILES)
            for q, (c, w) in enumerate(COLS):
                for f in range(KT):
                    job = ("gin", q, f)
                    product(job, bank(job)[:, 0:w],
                            [(H[:, s, f * P:(f + 1) * P], AT3[:, s, c:c + w]) for s in range(TILES)])
            pe.wait_ge(landed["w1"], 16)
            for q in range(NC3):
                for f in range(KT):
                    emptied(pe, ("gin", q, f))
            for h in range(8):
                for q, (c, w) in enumerate(COLS):
                    job = ("up", h, q)
                    product(job, bank(job)[:, 0:w],
                            [(w1[:, k, h * P:(h + 1) * P], HT[:, k, c:c + w]) for k in range(KT)])
            pe.wait_ge(landed["w2"], 16)
            pe.wait_ge(up_done, 8)
            for o in range(KT):
                for q, (c, w) in enumerate(COLS):
                    job = ("down", o, q)
                    product(job, bank(job)[:, 0:w],
                            [(w2[:, k, o * P:(o + 1) * P], UT[:, k, c:c + w]) for k in range(8)])
            pe.wait_ge(down_done, KT)
            for t in range(TILES + 2):
                if t < TILES:
                    job = ("gin_T", t)
                    b = take(job)
                    for f in range(KT):
                        mm = nc.tensor.transpose(b[0:TP, f * P:(f + 1) * P], HT[:, f, t * TP:(t + 1) * TP], ident[:, :])
                    fills(mm, job)
                if t >= 2:
                    pe.wait_ge(h3_ready, t - 1)
                    transposed(("h3_T", t - 2), t - 2)
            pe.wait_ge(landed["tv_w1"], 64)
            for t in range(TILES):
                emptied(pe, ("h3_T", t))
            for o in range(KT):
                for q, (c, w) in enumerate(COLS):
                    job = ("gate_hidden", o, q)
                    product(job, bank(job)[:, 0:w],
                            [(gfc1[:, k, o * P:(o + 1) * P], HT[:, k, c:c + w]) for k in range(KT)])
            pe.wait_ge(landed["ffn_small"], 48)
            pe.wait_ge(ghm_ready, 1)
            job = ("gates",)
            b = take(job)
            for k in range(KT):
                nc.tensor.matmul(b[:, 0:EXPERTS], ghmB[:, k, :], gfc2[:, k, :], start=(k == 0), stop=False)
            nc.tensor.matmul(b[:, 0:EXPERTS], ones[0:1, :], gfc2_b, start=False, stop=True)
            for k in range(KT):
                nc.tensor.matmul(b[0:EXPERTS, EXPERTS:EXPERTS + 1], gfc2[:, k, :], ghm[:, k:k + 1], start=(k == 0), stop=False)
            fills(nc.tensor.matmul(b[0:EXPERTS, EXPERTS:EXPERTS + 1], gfc2_b, ones[0:1, 0:1], start=False, stop=True), job)
            pe.wait_ge(g_ready, 1)
            for r in range(3):
                job = ("rows", r)
                product(job, bank(job)[0:TP, :], [(gB9[:, min(r, 1), :], tv_rows[:, FF + r * D:FF + (r + 1) * D])])
            job = ("b1m",)
            b = take(job)
            for m in range(2):
                mm = nc.tensor.matmul(b[:, m:m + 1], tv_rows[:, m * P:(m + 1) * P], g9[0:EXPERTS + 1, :], start=True, stop=True)
            fills(mm, job)
            pe.wait_ge(w1m_ready, 1)
            fw1 = ffn_w1.rearrange("p (k f) -> p k f", k=KT)
            fw2 = ffn_w2.rearrange("p (k n) -> p k n", k=2)
            for m in range(2):
                for q, (c, w) in enumerate(COLS):
                    job = ("ffn_hidden", m, q)
                    product(job, bank(job)[:, 0:w],
                            [(fw1[:, k, m * P:(m + 1) * P], HT[:, k, c:c + w]) for k in range(KT)])
            pe.wait_ge(w2m_ready, 1)
            for m in range(2):
                for q in range(NC3):
                    emptied(pe, ("ffn_hidden", m, q))
            for t in range(TILES):
                job = ("ffn_out", t)
                product(job, bank(job)[0:TP, :],
                        [(ffn_hidden[:, k, t * TP:(t + 1) * TP], fw2[:, k, :]) for k in range(2)])


def kernel(**inputs):
    import numpy as np
    import concourse.bacc as bacc
    from concourse.bass_utils import run_bass_kernel_spmd

    g = {k: np.asarray(v) for k, v in inputs.items()}

    def kxm(w):
        return np.ascontiguousarray(w.reshape(-1, P, w.shape[1]).transpose(1, 0, 2))

    pad = GROUPS * GROUP * P - EDGES

    def chunked(i, fill):
        return np.concatenate([i, np.full(pad, fill, np.int32)]).reshape(CHUNKS, P).T

    def cols(v):
        return v.reshape(-1, P).T

    f = {
        "x": g["x"],
        "edges": np.ascontiguousarray(np.concatenate([chunked(g["dst"], -1), chunked(g["src"], 0)], axis=1)),
        "edge_attr": np.concatenate([g["edge_attr_512"], np.zeros((pad, D), np.float32)]),
        "w_msg": kxm(g["L0_gnn_Wm"].T), "w_upd": kxm(g["L0_gnn_Wu"].T),
        "rows": np.stack([g["L0_gnn_bu"], g["L0_gnn_gamma"], g["L0_gnn_beta"]]),
        "vec": np.ascontiguousarray(np.concatenate([cols(g[n]) for n in (
            "L0_gnn_bm", "L0_ffn_b1_all", "L1_gnn_b1", "L1_gnn_g1", "L1_gnn_be1", "L1_gnn_b2", "L1_gnn_g2",
            "L1_gnn_be2", "L1_ffn_gfc1_b")], axis=1)),
        "eps": g["L1_gnn_eps"].reshape(1, 1),
        "router_w": kxm(g["L0_ffn_router_w"].T),
        "moe_w1": np.stack([kxm(w.T) for w in g["L0_ffn_w1_all"]]),
        "moe_w2": np.stack([kxm(w.T) for w in g["L0_ffn_w2_all"]]),
        "moe_b2": g["L0_ffn_b2_all"],
        "w1": kxm(g["L1_gnn_W1"]), "w2": kxm(g["L1_gnn_W2"]),
        "gfc1": kxm(g["L1_ffn_gfc1_w"].T), "gfc2": kxm(g["L1_ffn_gfc2_w"].T),
        "gfc2_b": g["L1_ffn_gfc2_b"].reshape(1, EXPERTS),
        "ffn_w1": kxm(g["L1_ffn_W1"].T).reshape(P, -1), "ffn_w2": kxm(g["L1_ffn_W2"].T).reshape(P, -1),
        "tv_w1": np.stack([kxm(w.T).reshape(P, -1) for w in g["L1_ffn_tv_W1"]], axis=1),
        "tv_w2": np.stack([kxm(w.T).reshape(P, -1) for w in g["L1_ffn_tv_W2"]], axis=1),
        "tv_rows": np.concatenate([np.concatenate([g["L1_ffn_tv_" + n], g["L1_ffn_" + n][None]]) for n in (
            "b1", "b2", "ln_g", "ln_b")], axis=1),
    }
    nc = bacc.Bacc("TRN2", target_bir_lowering=False, num_devices=1)
    aps = {n: nc.dram_tensor(f"in_{n}", v.shape, mybir.dt.from_np(v.dtype), kind="ExternalInput").ap()
           for n, v in f.items()}
    out = nc.dram_tensor("out", (NODES, D), F32, kind="ExternalOutput").ap()
    gnn_ffn_kernel(nc, aps, out)
    r = run_bass_kernel_spmd(nc, [{f"in_{n}": v for n, v in f.items()}], core_ids=[0])
    return r.results[0]["out"]
```

```python
from contextlib import ExitStack

import concourse.bass as bass
from concourse import mybir

F32 = mybir.dt.float32
F32R = mybir.dt.float32r
F16 = mybir.dt.float16
BF16 = mybir.dt.bfloat16
I32 = mybir.dt.int32
U32 = mybir.dt.uint32
ALU = mybir.AluOpType
ACT = mybir.ActivationFunctionType
AX = mybir.AxisListType.X

P = 128
NODES, D, EDGES = 1250, 512, 41250
TILES, TP = 10, 125
KT = D // P
GROUP = 4
GROUPS = -(-EDGES // (GROUP * P))
CHUNKS = GROUPS * GROUP
EXPERTS, FF = 8, 256
HID = 1024
EPS = 1e-5
MERGE = 0.03
COLS = [(0, 417), (417, 417), (834, 416)]
NC3 = len(COLS)
ADDED_LAST = 2
SPANS = [(0, 500), (500, 500), (1000, 250)]
F32R_INT = 4096
BANKS = 8

VEC = {}
_at = 0
for _name, _n in [("bm", 4), ("moe_b1", 16), ("b1", 8), ("g1", 8), ("be1", 8), ("b2", 4), ("g2", 4),
                  ("be2", 4), ("gfc1_b", 4)]:
    VEC[_name] = (_at, _at + _n)
    _at += _n
NVEC = _at


def psum_jobs():
    jobs = [("over",)]
    jobs += [("agg_in", 0, c, f) for c in range(NC3) for f in range(2)]
    jobs += [("deg", q) for q in range(3)]
    jobs += [("agg_in", 1, c, f) for c in range(NC3) for f in range(2)]
    jobs += [("joint_w", k) for k in range(KT)] + [("joint_b",)]
    for t in range(TILES + 2):
        if t < TILES:
            jobs.append(("update", t))
        if t == TILES:
            jobs.append(("router",))
        if t >= 2:
            jobs.append(("h1_T", t - 2))
    for e in range(EXPERTS):
        jobs += [("moe_hidden", e, m, c) for m in range(2) for c in range(NC3)]
        jobs += [("moe_out", e, t) for t in range(TILES)]
    jobs += [("gate_T", q) for q in range(3)]
    jobs += [("moe_bias", t) for t in range(TILES)]
    jobs += [("gin", r, c, f) for r in range(2) for c in range(NC3) for f in range(2)]
    jobs += [("up", h, c) for h in range(8) for c in range(NC3)]
    jobs += [("down", o, c) for o in range(KT) for c in range(NC3)]
    jobs += [("gin_T", t) for t in range(BANKS)] + h3_jobs()
    jobs += [("gates",)] + [("rows", r) for r in range(3)] + [("b1m",)]
    jobs += [("ffn_hidden", m, c) for m in range(2) for c in range(NC3)]
    jobs += [("ffn_out", t) for t in range(TILES)]
    return {job: n for n, job in enumerate(jobs)}


def h3_jobs():
    jobs = []
    hidden = [("gate_hidden", o, c) for c in range(NC3) for o in range(KT)]
    for t in range(TILES):
        jobs.append(("h3_T", t))
        if t + BANKS < TILES:
            jobs.append(("gin_T", t + BANKS))
        if hidden and (COLS[hidden[0][2]][0] + COLS[hidden[0][2]][1] - 1) // TP <= t:
            jobs.append(hidden.pop(0))
    return jobs + hidden


def norm_calls():
    calls = [("h0", t) for t in range(TILES)]
    for t in range(TILES):
        calls += [("update", t), ("x1", t)]
    calls += [("x2", t) for t in range(TILES)] + [("up", h) for h in range(8)] + [("down", h) for h in range(KT)]
    calls += [("x3", t) for t in range(TILES)] + [("y", t) for t in range(TILES)]
    return {call: n for n, call in enumerate(calls)}


def gnn_ffn_kernel(nc, a, out, counts):
    job_number = psum_jobs()
    norm_number = norm_calls()
    with ExitStack() as ctx:
        def sb(name, shape, dt=F32):
            return ctx.enter_context(nc.sbuf_tensor(name, shape, dt))

        def sem(name):
            return ctx.enter_context(nc.semaphore(name))

        XR = sb("X", [P, TILES * D])
        H = sb("H", [TP, TILES, D])
        HT = sb("HT", [P, KT, NODES])
        with nc.sbuf_tensor("AT", [P, TILES * NODES], F32R) as AT:
            pass
        late = sb("late", [P, TILES * NODES])
        U = sb("U", [P, 8 * NODES])
        W = sb("W", [P, 8192])
        rows = sb("rows", [TP, 3, D])
        hi = sb("hi", [P, GROUP, D], F32R)
        lo = sb("lo", [P, GROUP, D], F32R)
        dst_hot_r = sb("dst_hot_r", [P, GROUP, P], F32R)
        ident = sb("ident", [P, P])
        vec = sb("vec", [P, NVEC])
        small = sb("small", [P, 208])
        rng = sb("rng", [2, 16], I32)

        AT3 = AT[0:TP, :].rearrange("p (s n) -> p s n", s=TILES)

        def view(region, at, parts, *shape):
            n = 1
            for s in shape:
                n *= s
            v = region[0:parts, at:at + n]
            if len(shape) == 2:
                return v.rearrange("p (a b) -> p a b", a=shape[0])
            return v

        X = view(XR, 0, TP, TILES, D)
        ZT = view(U, 0, P, KT, NODES)
        UP = KT * NODES
        a_row = view(U, UP, TP, NODES)
        s_row = view(U, UP + 1250, TP, D)
        edge_rows = view(XR, 0, P, 2 * GROUP, D)
        src_hot = W[:, 3072:8072].bitcast(BF16).rearrange("p (s n) -> p s n", s=2 * GROUP)
        iota = U[:, UP + 3012:UP + 3637].bitcast(F16)
        dst_hot = XR[:, 4096:4608].bitcast(BF16).rearrange("p (s n) -> p s n", s=2 * GROUP)
        dst_f = view(U, UP + 3766, P, CHUNKS)
        src_f = view(U, UP + 4090, P, CHUNKS)
        ge = U[:, UP + 4414:UP + 4738].bitcast(BF16).rearrange("p (s n) -> p s n", s=2)
        idx = U[:, 0:2 * CHUNKS].bitcast(I32)
        first_g = view(U, 700, TILES, CHUNKS)
        last_g = view(U, 1100, TILES, CHUNKS)
        hit = view(U, 1500, TILES, CHUNKS)
        sign = U[:, 1900:1900 + 11].bitcast(BF16)
        joint_w = view(U, UP, P, KT, D)
        joint_b = view(W, 0, TP, D)
        bmB = view(W, 7424, P, KT, P)
        degB = view(W, 6144, P, NODES)
        recB = view(XR, 0, P, NODES)
        hidden = [view(U, s * 2 * NODES, P, 2, NODES) for s in range(2)]
        gateT = view(U, 0, EXPERTS, NODES)
        gate = view(U, UP + 2100, TP, TILES, EXPERTS)
        probs = view(U, UP + 2200, TP, TILES, EXPERTS)
        top_v = view(U, UP + 2300, TP, TILES, EXPERTS)
        top_i = U[0:TP, UP + 2400:UP + 2480].bitcast(U32).rearrange("p (t e) -> p t e", t=TILES)
        top_f = view(U, UP + 2500, TP, TILES, EXPERTS)
        pick = view(U, UP + 2600, TP, TILES, EXPERTS)
        pick2 = view(U, UP + 2700, TP, TILES, EXPERTS)
        iota8 = sb("iota8", [TP, EXPERTS])
        rtmp = view(U, UP + 2810, TP, TILES)
        rsum = view(U, UP + 2820, TP, TILES)
        rw = view(U, UP + 2840, TP, 2, TILES)
        moe_b2 = view(U, UP + 4100, EXPERTS, D)
        router_w = sb("router_w", [P, KT, EXPERTS])
        UT = view(U, 0, P, 8, NODES)
        eyeps = view(U, UP + 4700, TP, TP)
        w_msg = view(W, 0, P, KT, D)
        w_upd = view(W, 2048, P, 8, D)
        upd = [view(U, UP + 2048 + s * D, TP, D) for s in range(2)]
        act_out = [view(U, UP + 2048 + (2 + s) * D, TP, D) for s in range(2)]
        deg_eye = view(U, UP + 2500, TP, TILES, TP)
        moe_w1 = [view(U, UP + s * 1024, P, KT, FF) for s in range(2)]
        moe_w2 = [view(W, s * 1024, P, 2, D) for s in range(2)]
        w1 = view(W, 4096, P, KT, HID)
        w2 = view(W, 0, P, 8, D)
        tv_w1 = view(late, 0, P, EXPERTS, KT * FF)
        gfc1 = view(late, 8192, P, KT, D)
        ffn_w1 = view(late, 10240, P, KT * FF)
        ffn_w2 = view(late, 11264, P, 2 * D)
        tv_w2 = view(W, 0, P, EXPERTS, 2 * D)
        tv_rows = view(U, UP, EXPERTS + 1, FF + 3 * D)
        gfc2 = view(U, UP + 1800, P, KT, EXPERTS)
        gfc2_b = view(U, UP + 1840, 1, EXPERTS)
        gB9 = view(U, UP + 1900, EXPERTS + 1, 2, TP)
        ghmB = view(U, 4000, P, KT, P)
        ffn_hidden = view(U, 0, P, 2, NODES)
        hi_half, lo_half = (v[:, :, :].rearrange("p a (b d) -> p (a b) d", b=2) for v in (hi, lo))
        exact = [[view(XR, 1250 + s * 500, TP, 500) for s in range(2)], [view(U, 2500 + s * 500, TP, 500) for s in range(2)]]

        psum = [ctx.enter_context(nc.psum_tensor(f"psum{b}", [P, 512], F32)) for b in range(BANKS)]

        ln_st = sb("ln_st", [TP, TILES, 6])
        ln_mv = sb("ln_mv", [TP, TILES, 2])
        ln_rs = sb("ln_rs", [TP, TILES])
        ln_ve = sb("ln_ve", [TP, TILES])
        ln_nm = sb("ln_nm", [TP, TILES])
        ln_nb = sb("ln_nb", [TP, TILES])
        bn_scale = sb("bn_scale", [P, 12])
        bn_shift = sb("bn_shift", [P, 12])
        degp = sb("degp", [TP, 3, TILES])
        deg = sb("deg", [TP, TILES])
        high_deg = small[0:TP, 0:TILES]
        zeros = sb("zeros", [P, D], BF16)
        ch_stats = small[:, 16:34]
        ch_mv = small[:, 34:36]
        ch_rstd = small[:, 36:37]
        ch_ve = small[:, 37:38]
        minus_half = small[:, 38:39]
        no_bias = small[:, 39:40]
        gsum = small[:, 40:52]
        ghm = small[:, 52:56]
        gB = small[:, 56:64]
        g9 = small[:, 64:65]
        lnc = small[0:EXPERTS + 1, 65:66]
        b1m = small[:, 66:68]
        pair_b1 = small[:, 74:78]
        eps1 = small[0:TP, 68:69]
        eps_in = small[0:TP, 69:70]
        over_n = small[0:TP, 12:13]
        over = small[0:1, 13:14].bitcast(I32)
        last_first = small[0:TILES, 70:72]
        lo_n = small[0:TILES, 72:74]
        ones = small[:, 80:208]

        def Q(t):
            return job_number[t]

        idx_in, x_in, vec_in, wmsg_in, wupd_in, rows_in = (sem(n) for n in (
            "idx_in", "x_in", "vec_in", "wmsg_in", "wupd_in", "rows_in"))
        consts = sem("consts")
        dve, pool = sem("dve_step"), sem("pool_step")
        hits = sem("hits")
        hits_used = sem("hits_used")
        range_ready = sem("range_ready")
        range_T = sem("range_T")
        rng_ready = sem("rng_ready")
        h0_ready, h0_T, h0_copied = sem("h0_ready"), sem("h0_T"), sem("h0_copied")
        rows_landed = [sem(f"edge_rows_landed{j}") for j in range(GROUP)]
        hi_ready = [sem(f"hi_ready{j}") for j in range(GROUP)]
        lo_ready = [sem(f"lo_ready{j}") for j in range(GROUP)]
        hot_ready = [sem(f"hot_ready{j}") for j in range(GROUP)]
        chunk_done = [sem(f"chunk_done{j}") for j in range(GROUP)]
        dst_ready = [sem(f"dst_ready{j}") for j in range(GROUP)]
        a_copied, s_copied, a_T, s_T, aT_copied, sT_copied = (
            [sem(f"{n}{p}") for p in range(2)] for n in ("a_copied", "s_copied", "a_T", "s_T", "aT_copied", "sT_copied"))
        bank_full = [sem(f"bank_full{b}") for b in range(BANKS)]
        bank_free = [sem(f"bank_free{b}") for b in range(BANKS)]
        landed = {n: sem(f"{n}_landed") for n in (
            "router_w", "moe_b2", "w1", "w2", "tv_w1", "tv_w2", "ffn_small")}
        moe_in = [sem(f"moe_weights_landed{s}") for s in range(2)]
        deg_diag = sem("deg_diag")
        var_ready, inv_std_ready = sem("var_ready"), sem("inv_std_ready")
        mean_ready, bmB_ready = sem("mean_ready"), sem("bmB_ready")
        gelu_in, gelu_done = sem("gelu_in"), sem("gelu_done")
        h1_ready, pair_b1_set = sem("h1_ready"), sem("pair_b1_set")
        exp_done, gate_ready = sem("exp_done"), sem("gate_ready")
        xh_done, bias_done = sem("xh_done"), sem("bias_done")
        counts_stored = sem("counts_stored")
        over_in = sem("over_in")
        split_hi, split_lo, split_used = sem("split_hi"), sem("split_lo"), sem("split_used")
        exact_in = [sem(f"exact_counts_landed{s}") for s in range(2)]
        exact_used = [sem(f"exact_counts_used{s}") for s in range(2)]
        h2_ready, h3_ready = sem("h2_ready"), sem("h3_ready")
        up_norm, up_done = sem("up_norm"), sem("up_done")
        down_norm, down_done = sem("down_norm"), sem("down_done")
        ghm_ready, g_ready = sem("ghm_ready"), sem("g_ready")
        w1m_ready, w2m_ready, out_ready, stored = (sem(n) for n in (
            "w1m_ready", "w2m_ready", "out_ready", "stored"))
        shift_ready = sem("shift_ready")
        y_scaled, y_ready, last_ready = sem("y_scaled"), sem("y_ready"), sem("last_ready")

        def slots(eng, n, *rings):
            half = eng.snap((n % 2) * GROUP, min_val=0, max_val=GROUP)
            return [[ring[:, bass.ds(half + j, 1), :].rearrange("p a d -> p (a d)") for j in range(GROUP)]
                    for ring in rings]

        class Groups:

            def __init__(self, eng, one_tile):
                self.eng = eng
                self.done = eng.alloc_register("groups_done")
                self.first, self.end = eng.alloc_register("first"), eng.alloc_register("end")
                eng.wait_ge(rng_ready, 1)
                eng.reg_mov(self.done, 1)
                self.load(0)
                one_tile(self, 0, 0, 1)
                with eng.Fori(1, TILES // 2) as i:
                    one_tile(self, i * 2 - 1, 1, i)
                    one_tile(self, i * 2, 0, i + 1)
                one_tile(self, TILES - 1, 1, TILES // 2)

            def load(self, t):
                self.eng.reg_load(self.first, rng[0:1, bass.ds(t, 1)])
                self.eng.reg_load(self.end, rng[1:2, bass.ds(t, 1)])

            def walk(self, t, group, after_group0=None):
                eng = self.eng
                first = eng.snap(self.first, min_val=0, max_val=GROUPS - 3)
                end = eng.snap(self.end, min_val=3, max_val=GROUPS)

                def one(index, which):
                    group(index, eng.snap(self.done, min_val=1, max_val=GROUPS * TILES), which)
                    eng.reg_add(self.done, self.done, 1)

                one(first, 0)
                if after_group0:
                    after_group0()
                one(first + 1, 1)
                with eng.Fori(first + 2, end) as index:
                    one(index, None)
                if not isinstance(t, int) or t < TILES - 1:
                    self.load(t + 1)

        def full(eng, job, loops=0):
            n = Q(job)
            eng.wait_ge(bank_full[n % BANKS], loops + (n // BANKS + 1))

        def emptied(eng, job):
            n = Q(job)
            eng.wait_ge(bank_free[n % BANKS], n // BANKS + 1)

        def spans_under(c, w, spans):
            return [q for q, (c0, w0) in enumerate(spans) if c0 < c + w and c < c0 + w0]

        def bank(job):
            return psum[Q(job) % BANKS]

        def frees(ins, job):
            ins.then_inc(bank_free[Q(job) % BANKS], 1)

        def tile(ap, t):
            return ap[:, :, t * TP:(t + 1) * TP]

        def half_slot(eng, layer, k):
            n = layer * 2 * TILES + k
            if n >= 2 * GROUP:
                eng.wait_ge(split_used, n - 2 * GROUP + 1)
            return n % (2 * GROUP)

        def exact_blocks():
            n, loads = 0, 0
            for layer in range(2):
                for r in range(2):
                    for q, (c, w) in enumerate(SPANS):
                        yield layer, r, q, n, loads
                        n += TILES // 2
                        loads += TILES // 2 * (w // TP)

        block = ctx.enter_context(nc.Block())

        @block.sync
        def _(sp):
            sp.dma_start(idx, a["edges"]).then_inc(idx_in, 16)
            for t in range(TILES):
                sp.dma_start(H[:, t, :], a["x"][t * TP:(t + 1) * TP, :]).then_inc(x_in, 16)
            sp.dma_start(vec[:, :], a["vec"]).then_inc(vec_in, 16)
            sp.dma_start(eps_in, a["eps"].broadcast_to([TP, 1])).then_inc(vec_in, 16)
            sp.dma_start(router_w[:, :, :], a["router_w"]).then_inc(landed["router_w"], 16)
            sp.dma_start(w_msg, a["w_msg"]).then_inc(wmsg_in, 16)
            for r in range(3):
                sp.dma_start(rows[:, r, :], a["rows"][r:r + 1, :].broadcast_to([TP, D])).then_inc(rows_in, 16)

            def load_tile(groups, t, p, u):
                def group(index, n, which):
                    rows_in_slot, = slots(sp, n, edge_rows)
                    for j in range(GROUP):
                        sp.wait_ge(hi_ready[j], n)
                        sp.wait_ge(lo_ready[j], n)
                        sp.dma_start(rows_in_slot[j],
                                     a["edge_attr"][bass.ds(index * (GROUP * P) + j * P, P), :])\
                          .then_inc(rows_landed[j], 16)
                groups.walk(t, group)

            Groups(sp, load_tile)
            for p in range(2):
                sp.wait_ge(s_T[p], TILES // 2 + 1)
            sp.dma_start(w_upd, a["w_upd"]).then_inc(wupd_in, 16)

            sp.wait_ge(counts_stored, 16 * (TILES + 1))
            over_reg = sp.alloc_register("over")
            emptied(sp, ("over",))
            sp.reg_load(over_reg, over)

            def load_exact(layer):
                with sp.If(sp.snap(over_reg, min_val=0, max_val=NODES) > 0):
                    for l, r, q, n, loads in exact_blocks():
                        if l != layer:
                            continue
                        c, w = SPANS[q]
                        with sp.Fori(0, TILES // 2) as i:
                            froms = [sp.snap((i * 2 + s) * TP) for s in range(2)]
                            for s in range(2):
                                sp.wait_ge(exact_used[s], i + (n + 1))
                                for b in range(w // TP):
                                    sp.dma_start(exact[layer][s][:, b * TP:(b + 1) * TP],
                                                 counts[c + b * TP:c + (b + 1) * TP, bass.ds(froms[s], TP)]
                                                 .rearrange("n s -> s n"),
                                                 allow_slow_non_contiguous=True).then_inc(exact_in[s], 16)

            load_exact(0)
            sp.wait_ge(mean_ready, NC3 * KT)
            for t in range(TILES):
                sp.dma_start(X[:, t, :], a["x"][t * TP:(t + 1) * TP, :]).then_inc(x_in, 16)
            sp.wait_ge(gelu_in, TILES)
            for s in range(2):
                sp.dma_start(moe_w1[s], a["moe_w1"][s]).then_inc(moe_in[s], 16)
                sp.dma_start(moe_w2[s], a["moe_w2"][s]).then_inc(moe_in[s], 16)
            sp.dma_start(w1, a["w1"]).then_inc(landed["w1"], 16)
            sp.dma_start(moe_b2, a["moe_b2"]).then_inc(landed["moe_b2"], 16)
            with sp.Fori(0, EXPERTS // 2 - 1) as pair:
                for s in range(2):
                    full(sp, ("moe_out", s, TILES - 1), loops=pair * 4)
                    sp.dma_start(moe_w1[s], a["moe_w1"][bass.ds(pair * 2 + (2 + s), 1), :, :, :].rearrange("e p k f -> p (e k) f"))\
                      .then_inc(moe_in[s], 16)
                    sp.dma_start(moe_w2[s], a["moe_w2"][bass.ds(pair * 2 + (2 + s), 1), :, :, :].rearrange("e p k f -> p (e k) f"))\
                      .then_inc(moe_in[s], 16)
            full(sp, ("moe_out", EXPERTS - 1, TILES - 1))
            sp.dma_start(w2, a["w2"]).then_inc(landed["w2"], 16)
            full(sp, ("moe_bias", TILES - 1))
            load_exact(1)
            full(sp, ("gin", 1, NC3 - 1, 1))
            sp.dma_start(gfc1, a["gfc1"]).then_inc(landed["tv_w1"], 16)
            sp.dma_start(tv_w1, a["tv_w1"]).then_inc(landed["tv_w1"], 16)
            sp.dma_start(ffn_w1, a["ffn_w1"]).then_inc(landed["tv_w1"], 16)
            sp.dma_start(ffn_w2, a["ffn_w2"]).then_inc(landed["tv_w1"], 16)
            full(sp, ("down", KT - 1, NC3 - 1))
            sp.dma_start(tv_rows, a["tv_rows"]).then_inc(landed["ffn_small"], 16)
            sp.dma_start(gfc2, a["gfc2"]).then_inc(landed["ffn_small"], 16)
            sp.dma_start(gfc2_b, a["gfc2_b"]).then_inc(landed["ffn_small"], 16)
            sp.dma_start(tv_w2, a["tv_w2"]).then_inc(landed["tv_w2"], 16)
            for t in range(TILES):
                if t < TILES - ADDED_LAST:
                    sp.wait_ge(out_ready, t + 1)
                else:
                    sp.wait_ge(last_ready, t + 1 - (TILES - ADDED_LAST))
                sp.dma_start(out[t * TP:(t + 1) * TP, :], X[:, t, :]).then_inc(stored, 16)
            sp.wait_ge(stored, 16 * TILES)

        @block.gpsimd
        def _(pl):
            for j in range(0, GROUP, 2):
                pl.sem_inc(lo_ready[j], 2)
            pl.memset(ident[:, :], 0.0).then_inc(pool, 1)
            pl.memset(minus_half, -0.5).then_inc(pool, 1)
            pl.wait_ge(pool, 2)
            pl.affine_select(out=ident[:, :], in_=ident[:, :], compare_op=ALU.not_equal, fill=1.0, base=0,
                             pattern=[[-1, P]], channel_multiplier=1).then_inc(consts, 1)
            pl.iota(iota[:, :], pattern=[[1, NODES]], base=0, channel_multiplier=0,
                    allow_small_or_imprecise_dtypes=True).then_inc(consts, 1)
            pl.iota(first_g, pattern=[[-1, GROUPS], [0, GROUP]], base=GROUPS, channel_multiplier=0,
                    allow_small_or_imprecise_dtypes=True).then_inc(consts, 1)
            pl.iota(last_g, pattern=[[1, GROUPS], [0, GROUP]], base=1, channel_multiplier=0,
                    allow_small_or_imprecise_dtypes=True).then_inc(consts, 1)
            pl.iota(iota8[:, :], pattern=[[1, EXPERTS]], base=0, channel_multiplier=0,
                    allow_small_or_imprecise_dtypes=True).then_inc(consts, 1)
            pl.wait_ge(vec_in, 32)
            pl.tensor_scalar(eps1, eps_in, 1.0, None, ALU.add).then_inc(pool, 1)

            def inv_std(name, i):
                pl.wait_ge(var_ready, norm_number[name, i] + 1)
                if name in ("up", "down"):
                    o, v = ch_rstd, ch_ve
                else:
                    o, v = ln_rs[:, i:i + 1], ln_ve[:, i:i + 1]
                pl.tensor_tensor(o, v, minus_half[0:v.shape[0], :], ALU.pow).then_inc(inv_std_ready, 1)

            def scale_and_shift(name, t):
                inv_std(name, t)
                pl.wait_ge(inv_std_ready, norm_number[name, t] + 1)
                pl.tensor_tensor(ln_nb[:, t:t + 1], ln_nm[:, t:t + 1], ln_rs[:, t:t + 1], ALU.mult).then_inc(shift_ready, 1)

            for t in range(TILES):
                scale_and_shift("h0", t)
            def rest_tile(groups, t, p, u):
                def group(index, n, which):
                    rows_in_slot, = slots(pl, n, edge_rows)
                    for j in range(0, GROUP, 2):
                        pl.wait_ge(chunk_done[j], n + 1)
                        pl.wait_ge(hi_ready[j], n + 1)
                        pl.tensor_tensor(lo[:, j, :], rows_in_slot[j], hi[:, j, :].bitcast(F32),
                                         ALU.subtract).then_inc(lo_ready[j], 1)
                groups.walk(t, group)

            Groups(pl, rest_tile)

            for t in range(TILES):
                inv_std("update", t)
                inv_std("x1", t)
            full(pl, ("update", TILES - 1))
            pl.wait_ge(pool, 3)
            pl.tensor_scalar(eyeps, ident[0:TP, 0:TP], eps1, None, ALU.mult).then_inc(pool, 1)
            for t in range(TILES):
                scale_and_shift("x2", t)
            for t in range(TILES):
                pl.wait_ge(h2_ready, t + 1)
                pl.tensor_tensor(X[:, t, :], X[:, t, :], H[:, t, :], ALU.add).then_inc(xh_done, 1)
            for name, n_out in (("up", 8), ("down", KT)):
                for h in range(n_out):
                    inv_std(name, h)
            for t in range(TILES):
                scale_and_shift("x3", t)
            emptied(pl, ("rows", 0))
            emptied(pl, ("rows", 2))
            for t in range(TILES):
                pl.wait_ge(h3_ready, t + 1)
                emptied(pl, ("h3_T", t))
                pl.tensor_tensor(H[:, t, :], H[:, t, :], rows[:, 0, :], ALU.add).then_inc(bias_done, 1)
                pl.tensor_tensor(X[:, t, :], X[:, t, :], rows[:, 2, :], ALU.add).then_inc(bias_done, 1)
            for t in range(TILES + 1):
                if t < TILES:
                    inv_std("y", t)
                if 1 <= t <= TILES - ADDED_LAST:
                    pl.wait_ge(y_ready, t)
                    pl.tensor_tensor(X[:, t - 1, :], X[:, t - 1, :], H[:, t - 1, :], ALU.add).then_inc(out_ready, 1)

        @block.scalar
        def _(ac):
            for j in range(GROUP):
                ac.sem_inc(hi_ready[j], 1)
                ac.sem_inc(dst_ready[j], 1)
            ac.sem_inc(counts_stored, 16)
            for p in range(2):
                ac.sem_inc(a_copied[p], 3)
                ac.sem_inc(aT_copied[p], 3)
            ac.wait_ge(vec_in, 32)

            def normalized(layer, t, src, ready):
                ac.wait_ge(shift_ready, layer * TILES + t + 1)
                nc.scalar.activation(H[:, t, :], src, ACT.Identity, scale=ln_rs[:, t:t + 1],
                                     bias=ln_nb[:, t:t + 1]).then_inc(ready, 1)

            for t in range(TILES + 1):
                if t < TILES:
                    normalized(0, t, H[:, t, :], h0_ready)
                if t >= 1:
                    ac.wait_ge(h0_T, t)
                    nc.scalar.activation(tile(HT, t - 1), psum[4 + (t - 1) % 4][:, 0:KT * TP].rearrange("p (k n) -> p k n", k=KT),
                                         ACT.Copy).then_inc(h0_copied, 1)

            def copy_counts(q, p, u, t):
                c, w = COLS[q]
                nc.scalar.activation(a_row[:, c:c + w], psum[4 * p + 1 + q][0:TP, 0:w], ACT.Copy,
                                     accum_out=degp[:, q, bass.ds(t, 1)]).then_inc(a_copied[p], 1)

            def copy_counts_T(q, p, u, t):
                s = min(4, TILES - 4 * q)
                nc.scalar.activation(AT3[:, 4 * q:4 * q + s, bass.ds(t * TP, TP)],
                                     psum[4 * p + 1 + q][0:TP, 0:s * TP].rearrange("p (s n) -> p s n", s=s),
                                     ACT.Copy).then_inc(aT_copied[p], 1)

            def store_counts(at):
                ac.dma_start(counts[bass.ds(at, TP), :], a_row).then_inc(counts_stored, 16)

            def split_half(layer, k):
                r, s = divmod(k, TILES)
                at = half_slot(ac, layer, k)
                if layer * 2 * TILES + k >= 2 * GROUP:
                    ac.wait_ge(split_lo, layer * 2 * TILES + k - 2 * GROUP + 1)
                nc.scalar.activation(hi_half[0:TP, at, :], H[:, s, r * 256:(r + 1) * 256], ACT.Copy).then_inc(split_hi, 1)

            def split_tile(groups, t, p, u):
                before = not (isinstance(t, int) and t == 0)
                bp, bu = 1 - p, (u if p else u - 1)
                prev = t - 1
                if before:
                    prev_at = prev * TP if isinstance(t, int) else ac.snap(prev * TP)
                    stored_before = t * 16 if isinstance(t, int) else ac.snap(t * 16)

                def group(index, n, which):
                    rows_in_slot, hot = slots(ac, n, edge_rows, dst_hot)

                    def first_part(j):
                        ac.wait_ge(rows_landed[j], n * 16)
                        ac.wait_ge(chunk_done[j], n + 1)
                        nc.scalar.activation(hi[:, j, :], rows_in_slot[j], ACT.Copy).then_inc(hi_ready[j], 1)

                    def target(j):
                        ac.wait_ge(hot_ready[j], n + 1)
                        nc.scalar.activation(dst_hot_r[:, j, 0:TP], hot[j][:, 0:TP], ACT.Copy).then_inc(dst_ready[j], 1)

                    def move_previous(j):
                        if before and which == 0:
                            if j == 0:
                                ac.wait_ge(counts_stored, stored_before)
                                ac.wait_ge(chunk_done[GROUP - 1], n + 1)
                                ac.wait_ge(a_T[p], u)
                            copy_counts(j, bp, bu, prev)
                        if before and which == 1:
                            if j == 0:
                                ac.wait_ge(a_T[bp], bu + 1)
                                store_counts(prev_at)
                            copy_counts_T(j, bp, bu, prev)

                    first_part(0)
                    for j in range(GROUP):
                        if j < GROUP - 1:
                            first_part(j + 1)
                        target(j)
                        if j < 3:
                            move_previous(j)
                groups.walk(t, group)

            groups = Groups(ac, split_tile)
            ac.wait_ge(chunk_done[GROUP - 1], ac.snap(groups.done, min_val=1, max_val=GROUPS * TILES) + 1)
            ac.wait_ge(a_T[0], TILES // 2 + 1)
            ac.wait_ge(counts_stored, 16 * TILES)
            for q in range(3):
                copy_counts(q, 1, TILES // 2, TILES - 1)
            ac.wait_ge(a_T[1], TILES // 2 + 1)
            store_counts((TILES - 1) * TP)
            for q in range(3):
                copy_counts_T(q, 1, TILES // 2, TILES - 1)
            for k in range(TILES + 5):
                split_half(0, k)
            for q in range(3):
                w = min(4, TILES - 4 * q) * TP
                full(ac, ("deg", q))
                frees(nc.scalar.activation(degB[:, q * 500:q * 500 + w], bank(("deg", q))[:, 0:w], ACT.Copy), ("deg", q))
            for k in range(TILES + 5, 2 * TILES):
                split_half(0, k)
            ac.wait_ge(counts_stored, 16 * (TILES + 1))
            for k in range(KT):
                job = ("joint_w", k)
                full(ac, job)
                frees(nc.scalar.activation(joint_w[:, k, :], bank(job)[:, :], ACT.Copy), job)
            full(ac, ("joint_b",))
            frees(nc.scalar.activation(joint_b, bank(("joint_b",))[0:TP, :], ACT.Copy), ("joint_b",))
            for t in range(TILES + 2):
                if t < TILES:
                    ac.wait_ge(gelu_in, t + 1)
                    nc.scalar.activation(act_out[t % 2], upd[t % 2], ACT.Gelu).then_inc(gelu_done, 1)
                if t >= 2:
                    job = ("h1_T", t - 2)
                    full(ac, job)
                    frees(nc.scalar.activation(tile(HT, t - 2), bank(job)[:, 0:KT * TP].rearrange("p (k n) -> p k n", k=KT),
                                               ACT.Copy), job)
            emptied(ac, ("router",))
            nc.scalar.activation(probs, probs, ACT.Exp).then_inc(exp_done, 1)
            with ac.Fori(0, EXPERTS // 2) as pair:
                n = Q(("moe_hidden", 1, 1, NC3 - 1))
                ac.wait_ge(bank_free[n % BANKS], pair * 4 + (n // BANKS - 3))
                nc.scalar.activation(pair_b1, vec[:, bass.ds(pair * 4 + VEC["moe_b1"][0], 4)], ACT.Copy)\
                    .then_inc(pair_b1_set, 1)
                ac.wait_ge(pair_b1_set, pair + 1)
                for s in range(2):
                    for m in range(2):
                        for q, (c, w) in enumerate(COLS):
                            job = ("moe_hidden", s, m, q)
                            full(ac, job, loops=pair * 4)
                            frees(nc.scalar.activation(
                                hidden[s][:, m, c:c + w], bank(job)[:, 0:w], ACT.Relu,
                                bias=pair_b1[:, 2 * s + m:2 * s + m + 1]), job)
            for q in range(3):
                w = min(4, TILES - 4 * q) * TP
                job = ("gate_T", q)
                full(ac, job)
                frees(nc.scalar.activation(gateT[:, q * 500:q * 500 + w], bank(job)[0:EXPERTS, 0:w], ACT.Copy), job)
            for k in range(TILES + 5):
                for t in (0, 1) if k == 0 else (k + 1,):
                    if t < TILES:
                        normalized(1, t, X[:, t, :], h2_ready)
                if k < TILES:
                    ac.wait_ge(h2_ready, k + 1)
                split_half(1, k)
            for r in range(2):
                for q, (c, w) in enumerate(SPANS):
                    for f in range(2):
                        job = ("gin", r, q, f)
                        full(ac, job)
                        frees(nc.scalar.activation(HT[:, 2 * r + f, c:c + w], bank(job)[:, 0:w], ACT.Copy), job)
                if r == 0:
                    for k in range(TILES + 5, 2 * TILES):
                        split_half(1, k)
            for name, arr, n_out, normed, finished, off, bvec in (
                    ("up", UT, 8, up_norm, up_done, 0, "b1"), ("down", HT, KT, down_norm, down_done, 8, "b2")):
                b0 = VEC[bvec][0]
                for h in range(n_out + 1):
                    if h < n_out:
                        for q, (c, w) in enumerate(COLS):
                            job = (name, h, q)
                            full(ac, job)
                            frees(nc.scalar.activation(arr[:, h, c:c + w], bank(job)[:, 0:w], ACT.Identity,
                                                       bias=vec[:, b0 + h:b0 + h + 1]), job)
                    if h >= 1:
                        ac.wait_ge(normed, h)
                        nc.scalar.activation(arr[:, h - 1, :], arr[:, h - 1, :], ACT.Relu,
                                             scale=bn_scale[:, off + h - 1:off + h],
                                             bias=bn_shift[:, off + h - 1:off + h]).then_inc(finished, 1)
            g0 = VEC["gfc1_b"][0]
            for job in h3_jobs():
                if job[0] == "h3_T":
                    for t in (0, 1) if job[1] == 0 else (job[1] + 1,):
                        if t < TILES:
                            normalized(2, t, X[:, t, :], h3_ready)
                    full(ac, job)
                    frees(nc.scalar.activation(tile(HT, job[1]), bank(job)[:, 0:KT * TP].rearrange("p (k n) -> p k n", k=KT),
                                               ACT.Copy), job)
                if job[0] == "gate_hidden":
                    _, o, q = job
                    c, w = COLS[q]
                    full(ac, job)
                    nc.scalar.activation(bank(job)[:, 0:w], bank(job)[:, 0:w], ACT.Relu, bias=vec[:, g0 + o:g0 + o + 1],
                                         accum_out=gsum[:, 3 * o + q:3 * o + q + 1]).then_inc(bank_free[Q(job) % BANKS], 1)
            for r in range(3):
                full(ac, ("rows", r))
                frees(nc.scalar.activation(rows[:, r, :], bank(("rows", r))[0:TP, :], ACT.Copy), ("rows", r))
            full(ac, ("b1m",))
            frees(nc.scalar.activation(b1m, bank(("b1m",))[:, 0:2], ACT.Copy), ("b1m",))
            emptied(ac, ("b1m",))
            for m in range(2):
                for q, (c, w) in enumerate(COLS):
                    job = ("ffn_hidden", m, q)
                    full(ac, job)
                    frees(nc.scalar.activation(ffn_hidden[:, m, c:c + w], bank(job)[:, 0:w], ACT.Relu,
                                               bias=b1m[:, m:m + 1]), job)
            for t in range(TILES):
                ac.wait_ge(y_scaled, t + 1)
                ac.wait_ge(inv_std_ready, norm_number["y", t] + 1)
                nc.scalar.activation(H[:, t, :], H[:, t, :], ACT.Identity, scale=ln_rs[:, t:t + 1],
                                     bias=no_bias[0:TP, :]).then_inc(y_ready, 1)

        @block.vector
        def _(ve):
            for j in range(GROUP):
                ve.sem_inc(hot_ready[j], 1)
            for j in range(1, GROUP, 2):
                ve.sem_inc(lo_ready[j], 2)
            for p in range(2):
                ve.sem_inc(s_copied[p], 1)
                ve.sem_inc(sT_copied[p], 1)
            steps = [0]

            def did(ins):
                steps[0] += 1
                ins.then_inc(dve, 1)

            def settle():
                ve.wait_ge(dve, steps[0])

            def chain(ins):
                did(ins)
                settle()

            def layer_norm_stats(src, t, negated=False):
                chain(nc.vector.bn_stats(ln_st[:, t, :], src))
                chain(nc.vector.bn_aggr(ln_mv[:, t, :], ln_st[:, t, :]))
                if negated:
                    nc.vector.tensor_scalar(ln_nm[:, t:t + 1], ln_mv[:, t, 0:1], -1.0, None, ALU.mult)
                nc.vector.tensor_scalar(ln_ve[:, t:t + 1], ln_mv[:, t, 1:2], EPS, None, ALU.add).then_inc(var_ready, 1)

            def normalize(dst, src, name, t):
                ve.wait_ge(inv_std_ready, norm_number[name, t] + 1)
                return nc.vector.tensor_scalar(dst, src, ln_mv[:, t, 0:1], ln_rs[:, t:t + 1], ALU.subtract, ALU.mult)

            did(nc.vector.memset(sign[:, :], 0.0))
            did(nc.vector.memset(ones[:, :], 1.0))
            did(nc.vector.memset(zeros[:, :], 0.0))
            did(nc.vector.memset(g9[:, :], 1.0))
            did(nc.vector.memset(no_bias, 0.0))
            did(nc.vector.memset(lnc[:, :], 1.0 - EXPERTS * MERGE))
            settle()
            did(nc.vector.memset(sign[:, 10:11], 1.0))
            did(nc.vector.memset(sign[:, 9:10], -1.0))
            did(nc.vector.memset(lnc[0:EXPERTS, :], MERGE))
            ve.wait_ge(idx_in, 16)
            did(nc.vector.tensor_copy(dst_f, idx[:, 0:CHUNKS]))
            chain(nc.vector.tensor_copy(src_f, idx[:, CHUNKS:2 * CHUNKS]))
            for i in range(TILES + 1):
                if i >= 2:
                    ve.wait_ge(hits_used, i - 1)
                nc.vector.tensor_scalar(ge[:, i % 2, :], dst_f, float(i * TP), None, ALU.is_ge).then_inc(hits, 1)
            ve.wait_ge(hits_used, TILES + 1)
            ve.wait_ge(consts, 5)
            for c, g in ((0, first_g), (1, last_g)):
                chain(nc.vector.scalar_tensor_tensor(out=hit, in0=psum[0][0:TILES, 0:CHUNKS], scalar=0.0, in1=g,
                                                     op0=ALU.is_gt, op1=ALU.mult))
                chain(nc.vector.tensor_reduce(last_first[:, c:c + 1], hit, AX, ALU.max))
            chain(nc.vector.tensor_scalar(lo_n[:, 0:1], last_first[:, 0:1], -1.0, float(GROUPS), ALU.mult, ALU.add))
            chain(nc.vector.tensor_scalar(lo_n[:, 0:1], lo_n[:, 0:1], float(GROUPS - 3), None, ALU.min))
            nc.vector.scalar_tensor_tensor(out=lo_n[:, 1:2], in0=lo_n[:, 0:1], scalar=3.0, in1=last_first[:, 1:2],
                                           op0=ALU.add, op1=ALU.max).then_inc(range_ready, 1)
            ve.wait_ge(range_T, 1)
            nc.vector.tensor_copy(rng[:, 0:TILES], psum[1][0:2, 0:TILES]).then_inc(rng_ready, 1)

            ve.wait_ge(x_in, 16 * TILES)
            for t in range(TILES):
                layer_norm_stats(H[:, t, :], t, negated=True)


            def copy_sums(p, u):
                nc.vector.tensor_copy(s_row, psum[4 * p][0:TP, :]).then_inc(s_copied[p], 1)

            def copy_sums_T(p, t):
                nc.vector.tensor_copy(ZT[:, :, bass.ds(t * TP, TP)],
                                      psum[4 * p][:, 0:KT * TP].rearrange("p (k n) -> p k n", k=KT)).then_inc(sT_copied[p], 1)

            def hot_tile(groups, t, p, u):
                before = not (isinstance(t, int) and t == 0)
                bp, bu = 1 - p, (u if p else u - 1)
                prev = t - 1

                def group(index, n, which):
                    rows_in_slot, hot, hot_src = slots(ve, n, edge_rows, dst_hot, src_hot)

                    def one_hots(j):
                        ve.wait_ge(chunk_done[j], n)
                        at = index * GROUP + j
                        nc.vector.tensor_scalar(hot_src[j], iota[:, :], src_f[:, bass.ds(at, 1)], None, ALU.is_equal)
                        nc.vector.tensor_scalar(hot[j][:, 0:TP], iota[:, bass.ds(t * TP, TP)],
                                                dst_f[:, bass.ds(at, 1)], None, ALU.is_equal).then_inc(hot_ready[j], 1)

                    def rest_part(j):
                        ve.wait_ge(chunk_done[j], n + 1)
                        ve.wait_ge(hi_ready[j], n + 1)
                        nc.vector.tensor_tensor(lo[:, j, :], rows_in_slot[j], hi[:, j, :].bitcast(F32),
                                                ALU.subtract).then_inc(lo_ready[j], 1)

                    for j in range(GROUP):
                        one_hots(j)
                    rest_part(1)
                    if before and which == 0:
                        ve.wait_ge(chunk_done[GROUP - 1], n + 1)
                        ve.wait_ge(s_T[p], u)
                        copy_sums(bp, bu)
                    if before and which == 1:
                        ve.wait_ge(s_T[bp], bu + 1)
                        copy_sums_T(bp, prev)
                    rest_part(3)
                groups.walk(t, group)

            groups = Groups(ve, hot_tile)
            ve.wait_ge(chunk_done[GROUP - 1], ve.snap(groups.done, min_val=1, max_val=GROUPS * TILES) + 1)
            ve.wait_ge(s_T[0], TILES // 2 + 1)
            copy_sums(1, TILES // 2)
            for p in range(2):
                ve.wait_ge(a_copied[p], 3 * (TILES // 2 + 1))
            chain(nc.vector.tensor_tensor(deg[:, :], degp[:, 0, :], degp[:, 1, :], ALU.add))
            chain(nc.vector.tensor_tensor(deg[:, :], deg[:, :], degp[:, 2, :], ALU.add))
            chain(nc.vector.tensor_scalar(high_deg, deg[:, :], float(F32R_INT), None, ALU.is_gt))
            nc.vector.tensor_reduce(over_n, high_deg, AX, ALU.add).then_inc(over_in, 1)
            full(ve, ("over",))
            frees(nc.vector.tensor_copy(over, bank(("over",))[0:1, 0:1]), ("over",))
            ve.wait_ge(s_T[1], TILES // 2 + 1)
            copy_sums_T(1, TILES - 1)

            def split_half(layer, k):
                r, s = divmod(k, TILES)
                at = half_slot(ve, layer, k)
                ve.wait_ge(split_hi, layer * 2 * TILES + k + 1)
                nc.vector.tensor_tensor(lo_half[0:TP, at, :], H[:, s, r * 256:(r + 1) * 256],
                                        hi_half[0:TP, at, :].bitcast(F32), ALU.subtract).then_inc(split_lo, 1)

            for k in range(4):
                split_half(0, k)
            for p in range(2):
                ve.wait_ge(a_T[p], TILES // 2 + 1)
            nc.vector.tensor_tensor(deg_eye, ident[0:TP, 0:TP].unsqueeze(1).broadcast_to([TP, TILES, TP]),
                                    deg[:, :].unsqueeze(2).broadcast_to([TP, TILES, TP]), ALU.mult).then_inc(deg_diag, 1)
            some = degp[:, 0, :]
            chain(nc.vector.tensor_scalar(degp[:, 1, :], deg[:, :], 1.0, None, ALU.max))
            chain(nc.vector.reciprocal(degp[:, 1, :], degp[:, 1, :]))
            chain(nc.vector.tensor_tensor(some, deg[:, :], degp[:, 1, :], ALU.mult))
            ve.wait_ge(vec_in, 32)
            bm = vec[:, VEC["bm"][0]:VEC["bm"][1]]
            nc.vector.tensor_copy(bmB, bm.unsqueeze(2).broadcast_to([P, KT, P])).then_inc(bmB_ready, 1)
            for k in range(4, TILES + 5):
                split_half(0, k)
            for r in range(2):
                for q, (c, w) in enumerate(SPANS):
                    for f in range(2):
                        job = ("agg_in", r, q, f)
                        z = ZT[:, 2 * r + f, c:c + w]
                        full(ve, job)
                        frees(nc.vector.tensor_tensor(z, bank(job)[:, 0:w], z, ALU.add), job)
                if r == 0:
                    for k in range(TILES + 5, 2 * TILES):
                        split_half(0, k)
            for q in range(3):
                emptied(ve, ("deg", q))
            chain(nc.vector.tensor_scalar(recB, degB, 1.0, None, ALU.max))
            chain(nc.vector.reciprocal(recB, recB))
            for q, (c, w) in enumerate(COLS):
                for f in range(KT):
                    for span in spans_under(c, w, SPANS):
                        emptied(ve, ("agg_in", f // 2, span, f % 2))
                    nc.vector.tensor_tensor(ZT[:, f, c:c + w], ZT[:, f, c:c + w], recB[:, c:c + w], ALU.mult)\
                      .then_inc(mean_ready, 1)
            emptied(ve, ("joint_b",))
            ve.wait_ge(rows_in, 48)
            ve.wait_ge(x_in, 32 * TILES)
            for t in range(TILES + 2):
                g = act_out[(t - 1) % 2]
                if 1 <= t <= TILES:
                    ve.wait_ge(gelu_done, t)
                    chain(nc.vector.tensor_tensor(g, g, H[:, t - 1, :], ALU.add))
                    layer_norm_stats(g, t - 1)
                if t >= 2:
                    normalize(H[:, t - 2, :], X[:, t - 2, :], "x1", t - 2).then_inc(h1_ready, 1)
                if t < TILES:
                    job = ("update", t)
                    full(ve, job)
                    frees(nc.vector.scalar_tensor_tensor(out=upd[t % 2], in0=joint_b, scalar=some[:, t:t + 1],
                                                         in1=bank(job)[0:TP, :], op0=ALU.mult, op1=ALU.add), job)
                    emptied(ve, job)
                    nc.vector.tensor_tensor(upd[t % 2], upd[t % 2], rows[:, 0, :], ALU.add).then_inc(gelu_in, 1)
                if 1 <= t <= TILES:
                    x = X[:, t - 1, :]
                    chain(normalize(g, g, "update", t - 1))
                    chain(nc.vector.tensor_tensor(g, g, rows[:, 1, :], ALU.mult))
                    chain(nc.vector.tensor_tensor(g, g, rows[:, 2, :], ALU.add))
                    chain(nc.vector.tensor_tensor(x, x, g, ALU.add))
                    layer_norm_stats(x, t - 1)
            full(ve, ("router",))
            logits = bank(("router",))[0:TP, 0:TILES * EXPERTS].rearrange("p (t e) -> p t e", t=TILES)

            def per_node(v):
                return v.unsqueeze(2).broadcast_to([TP, TILES, EXPERTS])

            chain(nc.vector.tensor_reduce(rtmp, logits, AX, ALU.max))
            frees(nc.vector.tensor_tensor(probs, logits, per_node(rtmp), ALU.subtract), ("router",))
            ve.wait_ge(exp_done, 1)
            chain(nc.vector.tensor_reduce(rsum, probs, AX, ALU.add))
            chain(nc.vector.reciprocal(rsum, rsum))
            chain(nc.vector.tensor_tensor(probs, probs, per_node(rsum), ALU.mult))
            for t in range(TILES):
                did(nc.vector.max(top_v[:, t, :], probs[:, t, :]))
            settle()
            for t in range(TILES):
                did(nc.vector.max_index(top_i[:, t, :], top_v[:, t, :], probs[:, t, :]))
            did(nc.vector.tensor_tensor(rtmp, top_v[:, :, 0], top_v[:, :, 1], ALU.add))
            settle()
            did(nc.vector.tensor_copy(top_f, top_i))
            chain(nc.vector.tensor_scalar(rtmp, rtmp, 1e-9, None, ALU.add))
            chain(nc.vector.reciprocal(rtmp, rtmp))
            for k in range(2):
                did(nc.vector.tensor_tensor(rw[:, k, :], top_v[:, :, k], rtmp, ALU.mult))
            e8 = iota8[:, :].unsqueeze(1).broadcast_to([TP, TILES, EXPERTS])
            did(nc.vector.tensor_tensor(pick, e8, per_node(top_f[:, :, 0]), ALU.is_equal))
            chain(nc.vector.tensor_tensor(pick2, e8, per_node(top_f[:, :, 1]), ALU.is_equal))
            did(nc.vector.tensor_tensor(pick, pick, per_node(rw[:, 0, :]), ALU.mult))
            chain(nc.vector.tensor_tensor(pick2, pick2, per_node(rw[:, 1, :]), ALU.mult))
            nc.vector.tensor_tensor(gate, pick, pick2, ALU.add).then_inc(gate_ready, 1)
            ve.wait_ge(gate_ready, 1)
            with ve.Fori(0, EXPERTS // 2) as pair:
                for s in range(2):
                    for t in range(TILES):
                        job = ("moe_out", s, t)
                        full(ve, job, loops=pair * 4)
                        frees(nc.vector.scalar_tensor_tensor(
                            out=X[:, t, :], in0=bank(job)[0:TP, :], scalar=gate[:, t, bass.ds(pair * 2 + s, 1)],
                            in1=X[:, t, :], op0=ALU.mult, op1=ALU.add), job)
            for t in range(TILES + 1):
                if t < TILES:
                    job = ("moe_bias", t)
                    full(ve, job)
                    frees(nc.vector.tensor_tensor(X[:, t, :], bank(job)[0:TP, :], X[:, t, :], ALU.add), job)
                    emptied(ve, job)
                    layer_norm_stats(X[:, t, :], t, negated=True)
                if t >= 2:
                    split_half(1, t - 2)
            for k in range(TILES - 1, 2 * TILES):
                split_half(1, k)
            for name, arr, n_out, normed, off, gv, bv in (("up", UT, 8, up_norm, 0, "g1", "be1"),
                                                          ("down", HT, KT, down_norm, 8, "g2", "be2")):
                for h in range(n_out):
                    for q, (c, w) in enumerate(COLS):
                        emptied(ve, (name, h, q))
                        did(nc.vector.bn_stats(ch_stats[:, 6 * q:6 * q + 6], arr[:, h, c:c + w]))
                    settle()
                    chain(nc.vector.bn_aggr(ch_mv, ch_stats))
                    nc.vector.tensor_scalar(ch_ve, ch_mv[:, 1:2], EPS, None, ALU.add).then_inc(var_ready, 1)
                    ve.wait_ge(inv_std_ready, norm_number[name, h] + 1)
                    sc, sh = bn_scale[:, off + h:off + h + 1], bn_shift[:, off + h:off + h + 1]
                    g0, b0 = VEC[gv][0] + h, VEC[bv][0] + h
                    chain(nc.vector.tensor_tensor(sc, ch_rstd, vec[:, g0:g0 + 1], ALU.mult))
                    chain(nc.vector.tensor_tensor(sh, ch_mv[:, 0:1], sc, ALU.mult))
                    nc.vector.tensor_tensor(sh, vec[:, b0:b0 + 1], sh, ALU.subtract).then_inc(normed, 1)
            for t in range(TILES):
                job = ("gin_T", t)
                full(ve, job)
                ve.wait_ge(xh_done, t + 1)
                frees(nc.vector.tensor_tensor(X[:, t, :], bank(job)[0:TP, :], X[:, t, :], ALU.add), job)
                emptied(ve, job)
                layer_norm_stats(X[:, t, :], t, negated=True)
            for o in range(KT):
                for q in range(NC3):
                    emptied(ve, ("gate_hidden", o, q))
            chain(nc.vector.tensor_reduce(ghm, gsum.rearrange("p (o q) -> p o q", o=KT), AX, ALU.add))
            chain(nc.vector.tensor_scalar(ghm, ghm, 1.0 / NODES, None, ALU.mult))
            nc.vector.tensor_copy(ghmB, ghm.unsqueeze(2).broadcast_to([P, KT, P])).then_inc(ghm_ready, 1)
            full(ve, ("gates",))
            did(nc.vector.tensor_copy(gB, bank(("gates",))[:, 0:EXPERTS]))
            frees(nc.vector.tensor_copy(g9[0:EXPERTS, :], bank(("gates",))[0:EXPERTS, EXPERTS:EXPERTS + 1]), ("gates",))
            emptied(ve, ("gates",))
            settle()
            did(nc.vector.tensor_copy(gB9[:, 1, :], lnc.broadcast_to([EXPERTS + 1, TP])))
            nc.vector.tensor_copy(gB9[:, 0, :], g9[0:EXPERTS + 1, :].broadcast_to([EXPERTS + 1, TP])).then_inc(g_ready, 1)
            ve.wait_ge(landed["tv_w1"], 64)
            def hidden_half(v, m):
                return v.rearrange("p (k f) -> p k f", k=KT)[:, :, m * P:(m + 1) * P]

            merges = [(hidden_half(ffn_w1, m), [hidden_half(tv_w1[:, e, :], m) for e in range(EXPERTS)], w1m_ready)
                      for m in range(2)]
            merges.append((ffn_w2, [tv_w2[:, e, :] for e in range(EXPERTS)], w2m_ready))
            for w, tv, ready in merges:
                if ready is w2m_ready:
                    ve.wait_ge(landed["tv_w2"], 16)
                for e in range(EXPERTS):
                    ins = nc.vector.scalar_tensor_tensor(out=w, in0=tv[e], scalar=gB[:, e:e + 1], in1=w,
                                                         op0=ALU.mult, op1=ALU.add)
                    if e < EXPERTS - 1:
                        chain(ins)
                    else:
                        ins.then_inc(ready, 1)
            def residual(t):
                job = ("ffn_out", t)
                full(ve, job)
                ve.wait_ge(bias_done, 2 * t + 2)
                frees(nc.vector.tensor_tensor(H[:, t, :], bank(job)[0:TP, :], H[:, t, :], ALU.add), job)

            residual(0)
            for t in range(TILES):
                h = H[:, t, :]
                emptied(ve, ("ffn_out", t))
                did(nc.vector.bn_stats(ln_st[:, t, :], h))
                if t < TILES - 1:
                    residual(t + 1)
                settle()
                chain(nc.vector.bn_aggr(ln_mv[:, t, :], ln_st[:, t, :]))
                nc.vector.tensor_scalar(ln_ve[:, t:t + 1], ln_mv[:, t, 1:2], EPS, None, ALU.add).then_inc(var_ready, 1)
                nc.vector.scalar_tensor_tensor(out=h, in0=h, scalar=ln_mv[:, t, 0:1], in1=rows[:, 1, :],
                                               op0=ALU.subtract, op1=ALU.mult).then_inc(y_scaled, 1)
            for t in range(TILES - ADDED_LAST, TILES):
                ve.wait_ge(y_ready, t + 1)
                nc.vector.tensor_tensor(X[:, t, :], X[:, t, :], H[:, t, :], ALU.add).then_inc(last_ready, 1)

        @block.tensor
        def _(pe):
            for j in range(GROUP):
                pe.sem_inc(chunk_done[j], 2)
            for p in range(2):
                pe.sem_inc(a_T[p], 1)
                pe.sem_inc(s_T[p], 1)
            def take(job, loops=0):
                n = Q(job)
                if n >= BANKS:
                    pe.wait_ge(bank_free[n % BANKS], loops + n // BANKS)
                return psum[n % BANKS]

            def fills(ins, job):
                ins.then_inc(bank_full[Q(job) % BANKS], 1)

            def product(job, out_ap, pairs, loops=0):
                take(job, loops)
                for i, (l, r) in enumerate(pairs):
                    mm = nc.tensor.matmul(out_ap, l, r, start=(i == 0), stop=(i == len(pairs) - 1))
                fills(mm, job)

            for i in range(TILES + 1):
                pe.wait_ge(hits, i + 1)
                nc.tensor.matmul(psum[0][0:TILES, 0:CHUNKS], sign[:, 10 - i:20 - i], ge[:, i % 2, :],
                                 start=(i == 0), stop=(i == TILES)).then_inc(hits_used, 1)
            pe.wait_ge(consts, 1)
            pe.wait_ge(range_ready, 1)
            nc.tensor.transpose(psum[1][0:2, 0:TILES], lo_n, ident[0:TILES, 0:TILES]).then_inc(range_T, 1)
            for t in range(TILES):
                pe.wait_ge(h0_ready, t + 1)
                if t >= 4:
                    pe.wait_ge(h0_copied, t - 3)
                for f in range(KT):
                    mm = nc.tensor.transpose(psum[4 + t % 4][:, f * TP:(f + 1) * TP], H[:, t, f * P:(f + 1) * P],
                                             ident[0:TP, 0:TP])
                mm.then_inc(h0_T, 1)

            def turn(p, u):
                pe.wait_ge(a_copied[p], u * 3 + 3)
                for st in range(TILES):
                    mm = nc.tensor.transpose(psum[4 * p + 1 + st // 4][0:TP, (st % 4) * TP:(st % 4 + 1) * TP],
                                             a_row[:, st * TP:(st + 1) * TP], ident[0:TP, 0:TP])
                mm.then_inc(a_T[p], 1)
                pe.wait_ge(s_copied[p], u + 1)
                for f in range(KT):
                    mm = nc.tensor.transpose(psum[4 * p][:, f * TP:(f + 1) * TP], s_row[:, f * P:(f + 1) * P],
                                             ident[0:TP, 0:TP])
                mm.then_inc(s_T[p], 1)

            def sum_tile(groups, t, p, u):
                before = not (isinstance(t, int) and t == 0)
                pe.wait_ge(sT_copied[p], u)
                nc.tensor.matmul(psum[4 * p][0:TP, :], zeros[:, 0:TP], zeros[:, 0:D], start=True, stop=False,
                                 skip_group_check=True)
                pe.wait_ge(aT_copied[p], u * 3)
                for q, (c, w) in enumerate(COLS):
                    nc.tensor.matmul(psum[4 * p + 1 + q][0:TP, 0:w], zeros[:, 0:TP], zeros[:, 0:w], start=True, stop=False,
                                     skip_group_check=True)

                def group(index, n, which):
                    hot, hot_src = slots(pe, n, dst_hot, src_hot)
                    for j in range(GROUP):
                        pe.wait_ge(hot_ready[j], n + 1)
                        for q, (c, w) in enumerate(COLS):
                            nc.tensor.matmul(psum[4 * p + 1 + q][0:TP, 0:w], hot[j][:, 0:TP], hot_src[j][:, c:c + w],
                                             start=False, stop=False, skip_group_check=True)
                        pe.wait_ge(dst_ready[j], n + 1)
                        nc.tensor.matmul(psum[4 * p][0:TP, :], dst_hot_r[:, j, 0:TP], hi[:, j, :], start=False, stop=False,
                                         skip_group_check=True)
                        pe.wait_ge(lo_ready[j], n + 2)
                        nc.tensor.matmul(psum[4 * p][0:TP, :], dst_hot_r[:, j, 0:TP], lo[:, j, :], start=False, stop=False,
                                         skip_group_check=True).then_inc(chunk_done[j], 1)

                groups.walk(t, group, (lambda: turn(1 - p, u if p else u - 1)) if before else None)

            pe.wait_ge(h0_copied, TILES)
            Groups(pe, sum_tile)
            turn(1, TILES // 2)

            pe.wait_ge(sT_copied[0], TILES // 2 + 1)
            pe.wait_ge(over_in, 1)
            product(("over",), bank(("over",))[0:1, 0:1], [(over_n, ones[0:TP, 0:1])])
            for p in range(2):
                pe.wait_ge(aT_copied[p], 3 * (TILES // 2 + 1))
                pe.wait_ge(sT_copied[p], TILES // 2 + 1)
            over_reg = pe.alloc_register("over")
            emptied(pe, ("over",))
            pe.reg_load(over_reg, over)
            blocks = {(layer, r, q): (n, loads) for layer, r, q, n, loads in exact_blocks()}
            for s in range(2):
                pe.sem_inc(exact_used[s], 1)

            def counts_product(name, layer, r):
                many = pe.snap(over_reg, min_val=0, max_val=NODES)
                with pe.If(many == 0):
                    for s in range(TILES):
                        n = (layer * 2 + r) * TILES + s
                        for part, ready in ((hi_half, split_hi), (lo_half, split_lo)):
                            pe.wait_ge(ready, n + 1)
                            for f in range(2):
                                for q, (c, w) in enumerate(SPANS):
                                    job = (name, r, q, f)
                                    opens = s == 0 and part is hi_half
                                    b = take(job) if opens else bank(job)
                                    mm = nc.tensor.matmul(b[:, 0:w], part[0:TP, n % (2 * GROUP), f * P:(f + 1) * P],
                                                          AT3[:, s, c:c + w], start=opens, stop=False, skip_group_check=True)
                        mm.then_inc(split_used, 1)
                with pe.If(many > 0):
                    pe.sem_inc(split_used, TILES)
                    if layer == 1:
                        pe.wait_ge(h2_ready, TILES)
                    for q, (c, w) in enumerate(SPANS):
                        first, loads = blocks[layer, r, q]
                        for s in range(TILES):
                            pe.wait_ge(exact_in[s % 2], 16 * (loads + (s // 2 + 1) * (w // TP)))
                            for f in range(2):
                                job = (name, r, q, f)
                                b = take(job) if s == 0 else bank(job)
                                mm = nc.tensor.matmul(b[:, 0:w], H[:, s, (2 * r + f) * P:(2 * r + f + 1) * P],
                                                      exact[layer][s % 2][:, 0:w], start=(s == 0), stop=False,
                                                      skip_group_check=True)
                            mm.then_inc(exact_used[s % 2], 1)

            for r in range(2):
                counts_product("agg_in", 0, r)
                for q, (c, w) in enumerate(SPANS):
                    for f in range(2):
                        job = ("agg_in", r, q, f)
                        fills(nc.tensor.matmul(bank(job)[:, 0:1], zeros[:, 0:P], zeros[:, 0:1], start=False, stop=True,
                                               skip_group_check=True), job)
                if r == 0:
                    pe.wait_ge(deg_diag, 1)
                    for q in range(3):
                        job = ("deg", q)
                        b = take(job)
                        for i in range(min(4, TILES - 4 * q)):
                            mm = nc.tensor.matmul(b[:, i * TP:(i + 1) * TP], ones[0:TP, :], deg_eye[:, 4 * q + i, :],
                                                  start=True, stop=True)
                        fills(mm, job)
            pe.wait_ge(wmsg_in, 16)
            pe.wait_ge(wupd_in, 16)
            for i in range(KT):
                job = ("joint_w", i)
                product(job, bank(job)[:, :], [(w_msg[:, k, i * P:(i + 1) * P], w_upd[:, KT + k, :]) for k in range(KT)])
            pe.wait_ge(bmB_ready, 1)
            job = ("joint_b",)
            product(job, bank(job)[0:TP, :], [(bmB[:, k, 0:TP], w_upd[:, KT + k, :]) for k in range(KT)])
            for i in range(KT):
                emptied(pe, ("joint_w", i))

            def transposed(job, t):
                b = take(job)
                for f in range(KT):
                    mm = nc.tensor.transpose(b[:, f * TP:(f + 1) * TP], H[:, t, f * P:(f + 1) * P], ident[0:TP, 0:TP])
                fills(mm, job)

            def route(t):
                emptied(pe, ("h1_T", t))
                for k in range(KT):
                    mm = nc.tensor.matmul(bank(("router",))[0:TP, t * EXPERTS:(t + 1) * EXPERTS],
                                          HT[:, k, t * TP:(t + 1) * TP], router_w[:, k, :], start=(k == 0), stop=(k == KT - 1))
                return mm

            for t in range(TILES + 2):
                if t < TILES:
                    job = ("update", t)
                    pe.wait_ge(mean_ready, KT * (spans_under(t * TP, TP, COLS)[-1] + 1))
                    product(job, bank(job)[0:TP, :],
                            [(src[:, k, t * TP:(t + 1) * TP], w[:, k, :])
                             for src, w in ((HT, w_upd), (ZT, joint_w)) for k in range(KT)])
                if t == TILES:
                    pe.wait_ge(landed["router_w"], 16)
                    take(("router",))
                    for i in range(TILES - 3):
                        route(i)
                if t >= 2:
                    pe.wait_ge(h1_ready, t - 1)
                    transposed(("h1_T", t - 2), t - 2)
                if t == TILES:
                    route(TILES - 3)
            route(TILES - 2)
            fills(route(TILES - 1), ("router",))
            with pe.Fori(0, EXPERTS // 2) as pair:
                for s in range(2):
                    pe.wait_ge(moe_in[s], pair * 32 + 32)
                    for m in range(2):
                        for q, (c, w) in enumerate(COLS):
                            job = ("moe_hidden", s, m, q)
                            product(job, bank(job)[:, 0:w],
                                    [(moe_w1[s][:, k, m * P:(m + 1) * P], HT[:, k, c:c + w]) for k in range(KT)],
                                    loops=pair * 4)
                    for t in range(TILES):
                        job = ("moe_out", s, t)
                        for q in spans_under(t * TP, TP, COLS):
                            for m in range(2):
                                n = Q(("moe_hidden", s, m, q))
                                pe.wait_ge(bank_free[n % BANKS], pair * 4 + (n // BANKS + 1))
                        product(job, bank(job)[0:TP, :],
                                [(hidden[s][:, k, t * TP:(t + 1) * TP], moe_w2[s][:, k, :]) for k in range(2)],
                                loops=pair * 4)
            for q in range(3):
                job = ("gate_T", q)
                b = take(job)
                for i in range(min(4, TILES - 4 * q)):
                    mm = nc.tensor.transpose(b[0:EXPERTS, i * TP:(i + 1) * TP], gate[:, 4 * q + i, :], ident[0:TP, 0:TP])
                fills(mm, job)
            pe.wait_ge(landed["moe_b2"], 16)
            for q in range(3):
                emptied(pe, ("gate_T", q))
            for t in range(TILES):
                job = ("moe_bias", t)
                product(job, bank(job)[0:TP, :], [(gateT[:, t * TP:(t + 1) * TP], moe_b2)])
            for r in range(2):
                counts_product("gin", 1, r)
                pe.wait_ge(h2_ready, TILES)
                pe.wait_ge(pool, 4)
                for q, (c, w) in enumerate(SPANS):
                    for f in range(2):
                        job = ("gin", r, q, f)
                        for i in range(w // TP):
                            t = c // TP + i
                            mm = nc.tensor.matmul(bank(job)[:, i * TP:(i + 1) * TP], H[:, t, (2 * r + f) * P:(2 * r + f + 1) * P],
                                                  eyeps, start=False, stop=(i == w // TP - 1), skip_group_check=True)
                        fills(mm, job)
            pe.wait_ge(landed["w1"], 16)
            for h in range(8):
                for q, (c, w) in enumerate(COLS):
                    job = ("up", h, q)
                    if h == 0:
                        for span in spans_under(c, w, SPANS):
                            for r in range(2):
                                for f in range(2):
                                    emptied(pe, ("gin", r, span, f))
                    product(job, bank(job)[:, 0:w],
                            [(w1[:, k, h * P:(h + 1) * P], HT[:, k, c:c + w]) for k in range(KT)])
            pe.wait_ge(landed["w2"], 16)
            early = [("down", o, q) for o in range(2) for q in range(NC3)]
            for ks in (range(7), range(7, 8)):
                pe.wait_ge(up_done, ks[-1] + 1)
                for job in early:
                    _, o, q = job
                    c, w = COLS[q]
                    b = take(job) if ks[0] == 0 else bank(job)
                    for k in ks:
                        mm = nc.tensor.matmul(b[:, 0:w], w2[:, k, o * P:(o + 1) * P], UT[:, k, c:c + w],
                                              start=(k == 0), stop=(k == 7), skip_group_check=True)
                    if ks[-1] == 7:
                        fills(mm, job)
            for o in range(2, KT):
                for q, (c, w) in enumerate(COLS):
                    job = ("down", o, q)
                    product(job, bank(job)[:, 0:w],
                            [(w2[:, k, o * P:(o + 1) * P], UT[:, k, c:c + w]) for k in range(8)])

            def down_T(t, fs):
                for f in fs:
                    mm = nc.tensor.transpose(bank(("gin_T", t))[0:TP, f * P:(f + 1) * P], HT[:, f, t * TP:(t + 1) * TP],
                                             ident[:, :])
                return mm

            pe.wait_ge(down_done, KT - 1)
            for t in range(BANKS):
                take(("gin_T", t))
                down_T(t, range(KT - 1))
            pe.wait_ge(down_done, KT)
            for t in range(BANKS):
                fills(down_T(t, [KT - 1]), ("gin_T", t))
            pe.wait_ge(landed["tv_w1"], 64)
            for job in h3_jobs():
                if job[0] == "h3_T":
                    pe.wait_ge(h3_ready, job[1] + 1)
                    transposed(job, job[1])
                elif job[0] == "gin_T":
                    take(job)
                    fills(down_T(job[1], range(KT)), job)
                else:
                    _, o, q = job
                    c, w = COLS[q]
                    if o == 0:
                        for t in range((c + w - 1) // TP + 1):
                            emptied(pe, ("h3_T", t))
                    product(job, bank(job)[:, 0:w],
                            [(gfc1[:, k, o * P:(o + 1) * P], HT[:, k, c:c + w]) for k in range(KT)])
            pe.wait_ge(landed["ffn_small"], 48)
            pe.wait_ge(ghm_ready, 1)
            job = ("gates",)
            b = take(job)
            for k in range(KT):
                nc.tensor.matmul(b[:, 0:EXPERTS], ghmB[:, k, :], gfc2[:, k, :], start=(k == 0), stop=False)
            nc.tensor.matmul(b[:, 0:EXPERTS], ones[0:1, :], gfc2_b, start=False, stop=True)
            for k in range(KT):
                nc.tensor.matmul(b[0:EXPERTS, EXPERTS:EXPERTS + 1], gfc2[:, k, :], ghm[:, k:k + 1], start=(k == 0), stop=False)
            fills(nc.tensor.matmul(b[0:EXPERTS, EXPERTS:EXPERTS + 1], gfc2_b, ones[0:1, 0:1], start=False, stop=True), job)
            pe.wait_ge(g_ready, 1)
            for r in range(3):
                job = ("rows", r)
                product(job, bank(job)[0:TP, :], [(gB9[:, min(r, 1), :], tv_rows[:, FF + r * D:FF + (r + 1) * D])])
            job = ("b1m",)
            b = take(job)
            for m in range(2):
                mm = nc.tensor.matmul(b[:, m:m + 1], tv_rows[:, m * P:(m + 1) * P], g9[0:EXPERTS + 1, :], start=True, stop=True)
            fills(mm, job)
            fw1 = ffn_w1.rearrange("p (k f) -> p k f", k=KT)
            fw2 = ffn_w2.rearrange("p (k n) -> p k n", k=2)
            for m in range(2):
                pe.wait_ge(w1m_ready, m + 1)
                for q, (c, w) in enumerate(COLS):
                    job = ("ffn_hidden", m, q)
                    product(job, bank(job)[:, 0:w],
                            [(fw1[:, k, m * P:(m + 1) * P], HT[:, k, c:c + w]) for k in range(KT)])
            pe.wait_ge(w2m_ready, 1)
            for t in range(TILES):
                job = ("ffn_out", t)
                for q in spans_under(t * TP, TP, COLS):
                    for m in range(2):
                        emptied(pe, ("ffn_hidden", m, q))
                product(job, bank(job)[0:TP, :],
                        [(ffn_hidden[:, k, t * TP:(t + 1) * TP], fw2[:, k, :]) for k in range(2)])


def kernel(**inputs):
    import numpy as np
    import concourse.bacc as bacc
    from concourse.bass_utils import run_bass_kernel_spmd

    g = {k: np.asarray(v) for k, v in inputs.items()}

    def kxm(w):
        return np.ascontiguousarray(w.reshape(-1, P, w.shape[1]).transpose(1, 0, 2))

    pad = GROUPS * GROUP * P - EDGES

    def chunked(i, fill):
        return np.concatenate([i, np.full(pad, fill, np.int32)]).reshape(CHUNKS, P).T

    def cols(v):
        return v.reshape(-1, P).T

    f = {
        "x": g["x"],
        "edges": np.ascontiguousarray(np.concatenate([chunked(g["dst"], -1), chunked(g["src"], 0)], axis=1)),
        "edge_attr": np.concatenate([g["edge_attr_512"], np.zeros((pad, D), np.float32)]),
        "w_msg": kxm(g["L0_gnn_Wm"]), "w_upd": kxm(g["L0_gnn_Wu"].T),
        "rows": np.stack([g["L0_gnn_bu"], g["L0_gnn_gamma"], g["L0_gnn_beta"]]),
        "vec": np.ascontiguousarray(np.concatenate([cols(g[n]) for n in (
            "L0_gnn_bm", "L0_ffn_b1_all", "L1_gnn_b1", "L1_gnn_g1", "L1_gnn_be1", "L1_gnn_b2", "L1_gnn_g2",
            "L1_gnn_be2", "L1_ffn_gfc1_b")], axis=1)),
        "eps": g["L1_gnn_eps"].reshape(1, 1),
        "router_w": kxm(g["L0_ffn_router_w"].T),
        "moe_w1": np.stack([kxm(w.T) for w in g["L0_ffn_w1_all"]]),
        "moe_w2": np.stack([kxm(w.T) for w in g["L0_ffn_w2_all"]]),
        "moe_b2": g["L0_ffn_b2_all"],
        "w1": kxm(g["L1_gnn_W1"]), "w2": kxm(g["L1_gnn_W2"]),
        "gfc1": kxm(g["L1_ffn_gfc1_w"].T), "gfc2": kxm(g["L1_ffn_gfc2_w"].T),
        "gfc2_b": g["L1_ffn_gfc2_b"].reshape(1, EXPERTS),
        "ffn_w1": kxm(g["L1_ffn_W1"].T).reshape(P, -1), "ffn_w2": kxm(g["L1_ffn_W2"].T).reshape(P, -1),
        "tv_w1": np.stack([kxm(w.T).reshape(P, -1) for w in g["L1_ffn_tv_W1"]], axis=1),
        "tv_w2": np.stack([kxm(w.T).reshape(P, -1) for w in g["L1_ffn_tv_W2"]], axis=1),
        "tv_rows": np.concatenate([np.concatenate([g["L1_ffn_tv_" + n], g["L1_ffn_" + n][None]]) for n in (
            "b1", "b2", "ln_g", "ln_b")], axis=1),
    }
    nc = bacc.Bacc("TRN2", target_bir_lowering=False, num_devices=1)
    aps = {n: nc.dram_tensor(f"in_{n}", v.shape, mybir.dt.from_np(v.dtype), kind="ExternalInput").ap()
           for n, v in f.items()}
    out = nc.dram_tensor("out", (NODES, D), F32, kind="ExternalOutput").ap()
    counts = nc.dram_tensor("counts", (NODES, NODES), F32, kind="Internal").ap()
    gnn_ffn_kernel(nc, aps, out, counts)
    r = run_bass_kernel_spmd(nc, [{f"in_{n}": v for n, v in f.items()}], core_ids=[0])
    return r.results[0]["out"]
```
